# Optimizing a Trainium2 kernel written in Bass

```python
import numpy as np
import jax
import jax.numpy as jnp

def _softmax(x, axis=-1):
    return jax.nn.softmax(x, axis=axis)
def _gelu(x):
    return jax.nn.gelu(x, approximate=True)
def _silu(x):
    return jax.nn.silu(x)
def _sigmoid(x):
    return jax.nn.sigmoid(x)
def _layernorm(x, axis=-1, eps=1e-5):
    m = jnp.mean(x, axis=axis, keepdims=True)
    v = jnp.var(x, axis=axis, keepdims=True)
    return (x - m) / jnp.sqrt(v + eps)
def _scatter_add(tgt, idx, src, axis=0):
    return tgt.at[idx].add(src)
def _segment_sum(src, seg, n):
    return jax.ops.segment_sum(src, seg, n)

kernel_name = 'mk_adj_resnorm_d4_adj_256_602cfc'

def setup_inputs(seed: int = 0):
    np.random.seed(seed)
    _w = jnp.asarray
    def _rec_inputs():
        import jax
        import jax.numpy as jnp
        _gk = jax.random.key(seed)
        x = -0.000929 + 1 * jax.random.normal(jax.random.fold_in(_gk, 1), (4096, 256), jnp.float32)
        _a = jax.random.bernoulli(jax.random.fold_in(_gk, 2), 0.00390625, (4096, 4096))
        adj = _a.astype(jnp.int32)
        return x, adj
    x, adj = _rec_inputs()
    def _L0_gnn_setup():
        import jax, jax.numpy as jnp
        import numpy as np
        N, IN_DIM, OUT_DIM, HEADS = (4096, 256, 256, 4)
        HEAD_DIM = OUT_DIM // HEADS
        NEG_INF = -9000000000000000.0
        LN_EPS = 1e-05
        key = jax.random.key(seed)
        ks = jax.random.split(key, 8)
        x = jax.random.normal(ks[0], (N, IN_DIM), dtype=jnp.float32)
        adj = jax.random.randint(ks[1], (N, N), 0, 2, dtype=jnp.int32)
        W = jax.random.normal(ks[2], (HEADS, IN_DIM, HEAD_DIM), dtype=jnp.float32) * (1.0 / np.sqrt(IN_DIM))
        a1 = jax.random.normal(ks[3], (HEADS, HEAD_DIM), dtype=jnp.float32) * (1.0 / np.sqrt(2 * HEAD_DIM))
        a2 = jax.random.normal(ks[4], (HEADS, HEAD_DIM), dtype=jnp.float32) * (1.0 / np.sqrt(2 * HEAD_DIM))
        Wr = jax.random.normal(ks[5], (IN_DIM, OUT_DIM), dtype=jnp.float32) * (1.0 / np.sqrt(IN_DIM))
        br = jax.random.normal(ks[6], (OUT_DIM,), dtype=jnp.float32) * 0.01
        gamma = jnp.ones((OUT_DIM,), dtype=jnp.float32)
        beta = jnp.zeros((OUT_DIM,), dtype=jnp.float32)
        return {'x': x, 'adj': adj, 'W': W, 'a1': a1, 'a2': a2, 'Wr': Wr, 'br': br, 'gamma': gamma, 'beta': beta}
    _L0_gnn_all = _L0_gnn_setup()
    _L0_gnn_in = {k: v for k, v in _L0_gnn_all.items() if k in ('W', 'a1', 'a2', 'Wr', 'br', 'gamma', 'beta', )}
    del _L0_gnn_all

    def _L1_gnn_setup():
        import jax, jax.numpy as jnp
        import numpy as np
        N = 4096
        IN_F = 256
        OUT_F = 64
        HEADS = 4
        NEG_SLOPE = 0.2
        key = jax.random.key(seed)
        k1, k2, k3, k4 = jax.random.split(key, 4)
        x = jax.random.normal(k1, (N, IN_F), dtype=jnp.float32)
        W = jax.random.normal(k2, (HEADS, IN_F, OUT_F), dtype=jnp.float32) * (1.0 / np.sqrt(IN_F))
        a = jax.random.normal(k3, (HEADS, 2 * OUT_F), dtype=jnp.float32) * (1.0 / np.sqrt(2 * OUT_F))
        adj_matrix = jax.random.randint(k4, (N, N), 0, 2, dtype=jnp.int32)
        return {'x': x, 'W': W, 'a': a, 'adj_matrix': adj_matrix}
    _L1_gnn_all = _L1_gnn_setup()
    _L1_gnn_in = {k: v for k, v in _L1_gnn_all.items() if k in ('W', 'a', )}
    del _L1_gnn_all

    def _L2_gnn_setup():
        import jax, jax.numpy as jnp
        import numpy as np
        N, D = (8192, 256)
        NEG_BIG = -9000000000000000.0
        key = jax.random.key(seed)
        k1, k2, k3 = jax.random.split(key, 3)
        h = jax.random.normal(k1, (N, D), dtype=jnp.float32)
        adj = jax.random.randint(k2, (N, N), 0, 2, dtype=jnp.int32)
        bound = np.sqrt(6.0 / (2 * D + 1)).astype(np.float32)
        a = jax.random.uniform(k3, (2 * D, 1), dtype=jnp.float32, minval=-bound, maxval=bound)
        return {'h': h, 'adj': adj, 'a': a}
    _L2_gnn_all = _L2_gnn_setup()
    _L2_gnn_in = {k: v for k, v in _L2_gnn_all.items() if k in ('a', )}
    del _L2_gnn_all

    def _L3_gnn_setup():
        import jax, jax.numpy as jnp
        import numpy as np
        N = 8192
        D_IN = 256
        D_HID = 256
        D_OUT = 256
        key = jax.random.key(seed)
        k_x, k_a, k_q, k_k, k_v = jax.random.split(key, 5)
        X = jax.random.normal(k_x, (N, D_IN), dtype=jnp.float32)
        A = jax.random.randint(k_a, (N, N), 0, 2, dtype=jnp.int32)
        A = A * (1 - jnp.eye(N, dtype=jnp.int32))
        Wq = jax.random.normal(k_q, (D_IN, D_HID), dtype=jnp.float32) / 10.0
        Wk = jax.random.normal(k_k, (D_IN, D_HID), dtype=jnp.float32) / 10.0
        Wv = jax.random.normal(k_v, (D_IN, D_OUT), dtype=jnp.float32) / 10.0
        return {'X': X, 'A': A, 'Wq': Wq, 'Wk': Wk, 'Wv': Wv}
    _L3_gnn_all = _L3_gnn_setup()
    _L3_gnn_in = {k: v for k, v in _L3_gnn_all.items() if k in ('Wq', 'Wk', 'Wv', )}
    del _L3_gnn_all

    return {
        "x": x,
        "adj": adj,
        "L0_gnn_W": _L0_gnn_in["W"],
        "L0_gnn_a1": _L0_gnn_in["a1"],
        "L0_gnn_a2": _L0_gnn_in["a2"],
        "L0_gnn_Wr": _L0_gnn_in["Wr"],
        "L0_gnn_br": _L0_gnn_in["br"],
        "L0_gnn_gamma": _L0_gnn_in["gamma"],
        "L0_gnn_beta": _L0_gnn_in["beta"],
        "L1_gnn_W": _L1_gnn_in["W"],
        "L1_gnn_a": _L1_gnn_in["a"],
        "L2_gnn_a": _L2_gnn_in["a"],
        "L3_gnn_Wq": _L3_gnn_in["Wq"],
        "L3_gnn_Wk": _L3_gnn_in["Wk"],
        "L3_gnn_Wv": _L3_gnn_in["Wv"],
    }

def reference(x, adj, L0_gnn_W, L0_gnn_a1, L0_gnn_a2, L0_gnn_Wr, L0_gnn_br, L0_gnn_gamma, L0_gnn_beta, L1_gnn_W, L1_gnn_a, L2_gnn_a, L3_gnn_Wq, L3_gnn_Wk, L3_gnn_Wv):
    import jax
    import jax.numpy as jnp
    def _L0_gnn_ref(x, adj, W, a1, a2, Wr, br, gamma, beta):
        import jax, jax.numpy as jnp
        import numpy as np
        N, IN_DIM, OUT_DIM, HEADS = (4096, 256, 256, 4)
        HEAD_DIM = OUT_DIM // HEADS
        NEG_INF = -9000000000000000.0
        LN_EPS = 1e-05
        h = jnp.einsum('nd,hdk->hnk', x, W)
        s_col = jnp.einsum('hnk,hk->hn', h, a1)
        s_row = jnp.einsum('hnk,hk->hn', h, a2)
        e = jax.nn.leaky_relu(s_row[:, :, None] + s_col[:, None, :], negative_slope=0.2)
        e = jnp.where(adj[None, :, :] > 0, e, NEG_INF)
        att = jax.nn.softmax(e, axis=-1)
        h_prime = jnp.einsum('hij,hjk->hik', att, h)
        out = jnp.transpose(h_prime, (1, 0, 2)).reshape(N, OUT_DIM)
        residual = x @ Wr + br
        y = jax.nn.elu(out) + residual
        mu = jnp.mean(y, axis=-1, keepdims=True)
        var = jnp.var(y, axis=-1, keepdims=True)
        return gamma * (y - mu) / jnp.sqrt(var + LN_EPS) + beta

    def _L1_gnn_ref(x, W, a, adj_matrix):
        import jax, jax.numpy as jnp
        import numpy as np
        N = 4096
        IN_F = 256
        OUT_F = 64
        HEADS = 4
        NEG_SLOPE = 0.2
        heads, in_f, out_f = W.shape
        n = x.shape[0]
        xt = jnp.einsum('ni,hio->hno', x, W)
        src = jnp.einsum('hnf,hf->hn', xt, a[:, :out_f])
        dst = jnp.einsum('hnf,hf->hn', xt, a[:, out_f:])
        e = jax.nn.leaky_relu(src[:, :, None] + dst[:, None, :], NEG_SLOPE)
        mask = (adj_matrix > 0)[None, :, :]
        e = jnp.where(mask, e, -jnp.inf)
        attention = jax.nn.softmax(e, axis=2)
        h_prime = jnp.einsum('hij,hjf->hif', attention, xt)
        return h_prime.transpose(1, 0, 2).reshape(n, heads * out_f)

    def _L2_gnn_ref(h, adj, a):
        import jax, jax.numpy as jnp
        import numpy as np
        N, D = (8192, 256)
        NEG_BIG = -9000000000000000.0
        d = h.shape[1]
        h1 = h @ a[:d]
        h2 = h @ a[d:]
        e = jax.nn.leaky_relu(h1 + h2.T, negative_slope=0.01)
        attention = jnp.where(adj > 0, e, NEG_BIG)
        attention = jax.nn.softmax(attention, axis=1)
        return attention @ h

    def _L3_gnn_ref(X, A, Wq, Wk, Wv):
        import jax, jax.numpy as jnp
        import numpy as np
        N = 8192
        D_IN = 256
        D_HID = 256
        D_OUT = 256
        n = A.shape[0]
        Af = A.astype(X.dtype) + jnp.eye(n, dtype=X.dtype)
        Q = X @ Wq
        K = X @ Wk
        V = X @ Wv
        S = Q @ K.T
        mask = jnp.nan_to_num(-jnp.inf * (1.0 - Af), nan=0.0)
        P = jax.nn.softmax(S + mask, axis=1)
        return P @ V

    x = _layernorm(x + _L0_gnn_ref(x, adj, L0_gnn_W, L0_gnn_a1, L0_gnn_a2, L0_gnn_Wr, L0_gnn_br, L0_gnn_gamma, L0_gnn_beta), axis=-1)
    x = _layernorm(x + _L1_gnn_ref(x, L1_gnn_W, L1_gnn_a, adj), axis=-1)
    x = _layernorm(x + _L2_gnn_ref(x, adj, L2_gnn_a), axis=-1)
    x = _layernorm(x + _L3_gnn_ref(x, adj, L3_gnn_Wq, L3_gnn_Wk, L3_gnn_Wv), axis=-1)
    return x


_drawn_inputs = setup_inputs


def setup_inputs(seed=0):
    import zlib

    import numpy as np

    out = dict(_drawn_inputs(seed))
    spreads = {'L0_gnn_gamma': (1.0, 0.2), 'L0_gnn_beta': (0.0, 0.1)}
    factors = {}
    for name, (base, spread) in spreads.items():
        noise = np.random.default_rng([zlib.crc32(name.encode()), seed]).standard_normal(out[name].shape)
        drawn = base * np.exp(spread * noise) if base else spread * noise
        out[name] = jnp.asarray(drawn.astype(out[name].dtype))
    for name, factor in factors.items():
        out[name] = (out[name] * factor).astype(out[name].dtype)
    return out
```

```python
from contextlib import ExitStack

import concourse.bass as bass
from concourse import mybir

F32 = mybir.dt.float32
BF16 = mybir.dt.bfloat16
I32 = mybir.dt.int32
ALU = mybir.AluOpType
ACT = mybir.ActivationFunctionType
AX_X = mybir.AxisListType.X

P = 128
N = 4096
D = 256
HEADS = 4
F = D // HEADS
T = N // P
DC = D // P
PAIRS = HEADS // 2
BODY = T // 2
GROUPS = 4
GW = N // GROUPS
GT = GW // P
SCH = 512
BIG = 2.0 ** 100
LN_EPS = 1e-5
GAT_SLOPE = 0.2
ROW_SLOPE = 0.01


def wait(eng, sem, count):
    if isinstance(count, int) and count <= 0:
        return
    eng.wait_ge(sem, count)


def peeled(eng, n, body):
    body(0, first=True, last=False)
    with eng.Fori(1, n - 1) as i:
        body(i, first=False, last=False)
    body(n - 1, first=False, last=True)


class Semaphores:

    def __init__(self, sem, name):
        self.sem, self.name, self.made = sem, name, {}

    def __getitem__(self, what):
        if what not in self.made:
            self.made[what] = self.sem(f"{self.name}_{what}")
        return self.made[what]


class Buffers:
    pass


def constants(nc, b, sem):
    made = sem("const_made")
    with nc.Block() as block:
        @block.gpsimd
        def _(pool):
            nc.gpsimd.memset(b.ident[:], 0.0).then_inc(made, 1)
            nc.gpsimd.memset(b.halves[:], 0.0).then_inc(made, 1)
            nc.gpsimd.memset(b.diag_big[:], 0.0).then_inc(made, 1)
            nc.gpsimd.memset(b.big_col[:], BIG).then_inc(made, 1)
            nc.gpsimd.memset(b.minus_half[:], -0.5).then_inc(made, 1)
            pool.wait_ge(made, 5)
            nc.gpsimd.affine_select(out=b.ident[:], in_=b.ident[:], compare_op=ALU.not_equal, fill=1.0, base=0,
                                    pattern=[[-1, P]], channel_multiplier=1).then_inc(made, 1)
            nc.gpsimd.affine_select(out=b.diag_big[:], in_=b.diag_big[:], compare_op=ALU.not_equal, fill=BIG, base=0,
                                    pattern=[[-1, P]], channel_multiplier=1).then_inc(made, 1)
            nc.gpsimd.affine_select(out=b.halves[:], in_=b.halves[:], compare_op=ALU.not_equal, fill=1.0, base=0,
                                    pattern=[[-1, F]], channel_multiplier=1).then_inc(made, 1)
            pool.wait_ge(made, 8)
            nc.gpsimd.affine_select(out=b.halves[:], in_=b.halves[:], compare_op=ALU.not_equal, fill=1.0, base=-F,
                                    pattern=[[-1, F]], channel_multiplier=1).then_inc(made, 1)
            pool.wait_ge(made, 9)


def gat_weights(nc, b, sem, name, W, a_self, a_other):
    loaded, did = sem(f"{name}_w_loaded"), sem(f"{name}_w_did")
    with nc.Block() as block:
        @block.sync
        def _(sp):
            for c in range(DC):
                sp.dma_start(b.wx[:, c, 0:D].rearrange("p (h k) -> p h k", h=HEADS),
                             W[:, c * P:(c + 1) * P, :].rearrange("h p k -> p h k")).then_inc(loaded, 16)
            sp.dma_start(b.avec[:, 0, :].rearrange("p (h k) -> p h k", h=HEADS),
                         a_self.partition_broadcast(P)).then_inc(loaded, 16)
            sp.dma_start(b.avec[:, 1, :].rearrange("p (h k) -> p h k", h=HEADS),
                         a_other.partition_broadcast(P)).then_inc(loaded, 16)

        @block.vector
        def _(dve):
            dve.wait_ge(loaded, 16 * (DC + 2))
            n = 0
            for c in range(DC):
                for s in range(2):
                    if n:
                        dve.wait_ge(did, n)
                    nc.vector.tensor_tensor(b.wprod[:], b.wx[:, c, 0:D], b.avec[:, s, :], ALU.mult).then_inc(did, 1)
                    dve.wait_ge(did, n + 1)
                    nc.vector.tensor_reduce(b.wsum[:, c, s, :], b.wprod[:].rearrange("p (h k) -> p h k", h=HEADS),
                                            AX_X, ALU.add).then_inc(did, 1)
                    n += 2
            dve.wait_ge(did, n)
            for c in range(DC):
                nc.vector.tensor_scalar(b.wx[:, c, D:D + HEADS], b.wsum[:, c, 0, :], -(1 - GAT_SLOPE), None,
                                        ALU.mult).then_inc(did, 1)
                nc.vector.tensor_scalar(b.wrow[:, c, 0:HEADS], b.wsum[:, c, 1, :], -1.0, None,
                                        ALU.mult).then_inc(did, 1)
                nc.vector.tensor_scalar(b.wrow[:, c, HEADS:2 * HEADS], b.wsum[:, c, 1, :], -GAT_SLOPE, None,
                                        ALU.mult).then_inc(did, 1)
            dve.wait_ge(did, n + 3 * DC)


def row_weights(nc, b, sem, name, a):
    loaded, did = sem(f"{name}_w_loaded"), sem(f"{name}_w_did")
    with nc.Block() as block:
        @block.sync
        def _(sp):
            sp.dma_start(b.wsum[:].rearrange("p c s h -> p (c s h)")[:, 0:2 * DC],
                         a.rearrange("(s p) one -> p (s one)", p=P), allow_slow_non_contiguous=True).then_inc(loaded, 16)

        @block.vector
        def _(dve):
            dve.wait_ge(loaded, 16)
            cols = b.wsum[:].rearrange("p c s h -> p (c s h)")
            for c in range(DC):
                nc.vector.tensor_scalar(b.wx[:, c, D:D + 1], cols[:, c:c + 1], -(1 - ROW_SLOPE), None,
                                        ALU.mult).then_inc(did, 1)
                nc.vector.tensor_scalar(b.wrow[:, c, 0:1], cols[:, DC + c:DC + c + 1], -1.0, None,
                                        ALU.mult).then_inc(did, 1)
                nc.vector.tensor_scalar(b.wrow[:, c, 1:2], cols[:, DC + c:DC + c + 1], -ROW_SLOPE, None,
                                        ALU.mult).then_inc(did, 1)
            dve.wait_ge(did, 3 * DC)


def dense_weights(nc, b, sem, name, pairs):
    loaded = sem(f"{name}_dense_loaded")
    with nc.Block() as block:
        @block.sync
        def _(sp):
            for dst, src in pairs:
                if len(src.shape) == 1:
                    sp.dma_start(dst, src.partition_broadcast(P)).then_inc(loaded, 16)
                else:
                    sp.dma_start(dst, src.rearrange("(c p) n -> p c n", p=P)).then_inc(loaded, 16)
            sp.wait_ge(loaded, 16 * len(pairs))


def tiles_of_rows(nc, b, sem, name, x_in, x_out, prev, kind):
    s = Semaphores(sem, name)
    fin = prev is not None
    n_in = 1 + (prev is not None) + (prev == 0)
    steps = {None: 0, 0: 12, 1: 4, 2: 4, 3: 4}[prev]
    powers = {None: 0, 0: 2, 1: 1, 2: 1, 3: 1}[prev]
    n_proj = {"gat": D + HEADS, "row": 1, "qkv": D, None: 0}[kind]
    n_rows = {"gat": 2 * HEADS, "row": 2}.get(kind, 0)
    xin = x_in.rearrange("(t p) d -> t p d", p=P)
    o_in = b.o_dram.rearrange("(t p) d -> t p d", p=P)
    res_in = b.res_dram.rearrange("(t p) d -> t p d", p=P)
    xo = None if x_out is None else x_out.rearrange("(t p) d -> t p d", p=P)

    with nc.Block() as block:
        @block.sync
        def _(sp):
            def body(i, first, last):
                for k in range(2):
                    t = sp.snap(i * 2 + k) if not isinstance(i, int) else i * 2 + k
                    if fin:
                        wait(sp, s["fin"], (i - 1) * 2 * steps + (k + 1) * steps if not first else 0)
                        if prev == 0:
                            pass
                    elif not first:
                        sp.wait_ge(s["xT_psum"], (i - 1) * 2 + k + 1)
                    dst = b.x_old if fin else b.xs
                    sp.dma_start(dst[:, k, :], xin[t, :, :]).then_inc(s[f"in{k}"], 16)
                    if fin:
                        sp.dma_start(b.o_tile[:, k, :], o_in[t, :, :]).then_inc(s[f"in{k}"], 16)
                    if prev == 0:
                        sp.dma_start(b.res_tile[:, k, :], res_in[t, :, :]).then_inc(s[f"in{k}"], 16)
            peeled(sp, BODY, body)

        def at(tile, buf, *rest):
            if isinstance(tile, int):
                return buf[(slice(None), slice(tile, tile + 1)) + rest]
            return buf[(slice(None), bass.ds(tile, 1)) + rest]

        def one(ap):
            return ap.rearrange("p (o n) -> p o n", o=1)

        @block.vector
        def _(dve):
            def finish(i, k, first):
                tile = i * 2 + k
                n = [0]

                def step(ins):
                    n[0] += 1
                    ins.then_inc(s["fin"], 1)
                    dve.wait_ge(s["fin"], tile * steps + n[0])

                def norm_stats(src):
                    step(nc.vector.bn_stats(b.stats[:, k, :], src))
                    dve.sem_inc(b.passed_dve, 1)
                    step(nc.vector.bn_aggr(b.mv[:, k, 0:2], b.stats[:, k, :]))

                dve.wait_ge(s[f"in{k}"], (i + 1) * 16 * n_in)
                z = b.z[:, k, :]
                if prev == 0:
                    step(nc.vector.tensor_scalar(z, b.o_tile[:, k, :], 0.0, None, ALU.min))
                    dve.wait_ge(s["elu"], tile + 1)
                    step(nc.vector.scalar_tensor_tensor(z, b.o_tile[:, k, :], 0.0, b.elu[:, k, :],
                                                        ALU.max, ALU.add))
                    step(nc.vector.scalar_tensor_tensor(z, z, -1.0, b.res_tile[:, k, :], ALU.add, ALU.add))
                    norm_stats(z)
                    dve.wait_ge(s["power"], tile * powers + 1)
                    step(nc.vector.tensor_scalar(z, z, b.mv[:, k, 0:1], b.mv[:, k, 3:4], ALU.subtract, ALU.mult))
                    step(nc.vector.tensor_tensor(z, z, b.gamma[:], ALU.mult))
                    step(nc.vector.tensor_tensor(z, z, b.beta[:], ALU.add))
                    step(nc.vector.tensor_tensor(z, z, b.x_old[:, k, :], ALU.add))
                else:
                    step(nc.vector.tensor_tensor(z, b.o_tile[:, k, :], b.x_old[:, k, :], ALU.add))
                norm_stats(z)
                dve.wait_ge(s["power"], tile * powers + powers)
                if not first:
                    if kind is not None:
                        dve.wait_ge(s["xT_psum"], (i - 1) * 2 + k + 1)
                    dve.wait_ge(s[f"x_kept{k}"], 16 * i)
                step(nc.vector.tensor_scalar(b.xs[:, k, :], z, b.mv[:, k, 0:1], b.mv[:, k, 3:4],
                                             ALU.subtract, ALU.mult))
                if kind == "row":
                    nc.vector.tensor_copy(at(tile, b.V, slice(None)), one(b.xs[:, k, :])).then_inc(s["x_value"], 1)

            def take(tile, k, i, fresh):
                dve.wait_ge(s["proj"], tile + 1)
                if kind == "row":
                    nc.vector.tensor_copy(at(tile, b.col, slice(0, 1)),
                                          one(b.bank[2 + k][:, D:D + 1])).then_inc(s["proj_out"], 1)
                    return
                if kind == "gat":
                    nc.vector.tensor_copy(at(tile, b.col, slice(None)), one(b.bank[2 + k][:, D:D + HEADS]))
                nc.vector.tensor_copy(at(tile, b.V, slice(None)), one(b.bank[2 + k][:, 0:D])).then_inc(s["proj_out"], 1)
                if kind == "qkv":
                    dve.wait_ge(s["res"], tile + 1)
                    dst = (b.KT[:, :, tile * P:(tile + 1) * P] if isinstance(tile, int)
                           else b.KT[:, :, bass.ds(tile * P, P)])
                    nc.vector.tensor_copy(dst, b.bank[6 + k][:, 0:D].rearrange("p (c n) -> p c n",
                                                                              c=DC)).then_inc(s["res_out"], 1)
                elif prev is None:
                    dve.wait_ge(s["res"], tile + 1)
                    wait(dve, s[f"res_kept{k}"], 16 * i)
                    nc.vector.tensor_tensor(b.res_tile[:, k, :], b.bank[6 + k][:, 0:D], b.br[:],
                                            ALU.add).then_inc(s["res_out"], 1)

            def body(i, first, last):
                for k in range(2):
                    tile = i * 2 + k
                    if fin:
                        finish(i, k, first)
                    if kind is not None and not (first and k == 0):
                        take(tile - 1, 1 - k, i if k == 1 else i - 1, (first and k == 1) or (isinstance(i, int) and i == 1 and k == 0))
            peeled(dve, BODY, body)
            if kind is not None:
                take(T - 1, 1, BODY - 1, False)

        @block.gpsimd
        def _(pool):
            if fin:
                def body(i, first, last):
                    for k in range(2):
                        tile = i * 2 + k
                        for w in range(powers):
                            done = {(0, 0): 5, (0, 1): 11}.get((prev, w), 3)
                            pool.wait_ge(s["fin"], tile * steps + done)
                            pool.sem_inc(b.passed_pool, 1)
                            nc.gpsimd.tensor_scalar(b.mv[:, k, 2:3], b.mv[:, k, 1:2], LN_EPS, None,
                                                    ALU.add).then_inc(s["var_eps"], 1)
                            pool.wait_ge(s["var_eps"], tile * powers + w + 1)
                            nc.gpsimd.tensor_tensor(b.mv[:, k, 3:4], b.mv[:, k, 2:3], b.minus_half[:],
                                                    ALU.pow).then_inc(s["power"], 1)
                peeled(pool, BODY, body)

        @block.scalar
        def _(act):
            def rows(tile, k, i, fresh):
                t = tile if isinstance(tile, int) else act.snap(tile)
                act.wait_ge(s["rows"], tile + 1)
                wait(act, s[f"rows_kept{k}"], 16 * i)
                if kind == "qkv":
                    nc.scalar.activation(b.qT[:, k, :, :], b.bank[4 + k][:, 0:D].rearrange("p (c n) -> p c n", c=DC),
                                         ACT.Copy, scale=-1.0).then_inc(s["rows_out"], 1)
                    act.wait_ge(s["rows_out"], tile + 1)
                    act.dma_start(b.q_dram[t, :, :, :], b.qT[:, k, :, :]).then_inc(s[f"rows_kept{k}"], 16)
                else:
                    nc.scalar.activation(b.row_tile[0:n_rows, k, :], b.bank[4 + k][0:n_rows, 0:P],
                                         ACT.Copy).then_inc(s["rows_out"], 1)
                    act.wait_ge(s["rows_out"], tile + 1)
                    act.dma_start(b.rows_dram.rearrange("r (t n) -> t r n", n=P)[t, 0:n_rows, :],
                                  b.row_tile[0:n_rows, k, :]).then_inc(s[f"rows_kept{k}"], 16)
                if prev is None:
                    act.wait_ge(s["res_out"], tile + 1)
                    act.dma_start(res_in[t, :, :], b.res_tile[:, k, :]).then_inc(s[f"res_kept{k}"], 16)

            def body(i, first, last):
                for k in range(2):
                    tile = i * 2 + k
                    t = act.snap(tile) if not isinstance(i, int) else tile
                    if prev == 0:
                        act.wait_ge(s["fin"], tile * steps + 1)
                        nc.scalar.activation(b.elu[:, k, :], b.z[:, k, :], ACT.Exp).then_inc(s["elu"], 1)
                    if fin:
                        act.wait_ge(s["fin"], (tile + 1) * steps)
                        act.dma_start(xo[t, :, :], b.xs[:, k, :]).then_inc(s[f"x_kept{k}"], 16)
                    if kind is None:
                        continue
                    act.wait_ge(s["xT_psum"], tile + 1)
                    if not first:
                        act.wait_ge(s["res"] if (kind == "qkv" or prev is None) else s["rows"], (i - 1) * 2 + k + 1)
                    nc.scalar.activation(b.xT[:, k, :, :], b.bank[k][:, 0:D].rearrange("p (c n) -> p c n", c=DC),
                                         ACT.Copy).then_inc(s["xT_sbuf"], 1)
                    if not (first and k == 0):
                        rows(tile - 1, 1 - k, i if k == 1 else i - 1, (first and k == 1) or (isinstance(i, int) and i == 1 and k == 0))
            peeled(act, BODY, body)
            if kind is not None:
                rows(T - 1, 1, BODY - 1, False)
            for k in range(2):
                if fin:
                    act.wait_ge(s[f"x_kept{k}"], 16 * BODY)
                if kind is not None:
                    act.wait_ge(s[f"rows_kept{k}"], 16 * BODY)
                if prev is None:
                    act.wait_ge(s[f"res_kept{k}"], 16 * BODY)

        if kind is not None:
            @block.tensor
            def _(pe):
                def project(tile, k, i, fresh):
                    pe.wait_ge(s["xT_sbuf"], tile + 1)
                    wait(pe, s["proj_out"], tile - 1)
                    a, z = (D, D + 1) if kind == "row" else (0, n_proj)
                    for c in range(DC):
                        mm = nc.tensor.matmul(b.bank[2 + k][:, a:z], b.xT[:, k, c, :], b.wx[:, c, a:z],
                                              start=c == 0, stop=c == DC - 1)
                    mm.then_inc(s["proj"], 1)
                    wait(pe, s["rows_out"], tile - 1)
                    if kind == "qkv":
                        for half in range(DC):
                            for c in range(DC):
                                mm = nc.tensor.matmul(b.bank[4 + k][:, half * P:(half + 1) * P],
                                                      b.wq[:, c, half * P:(half + 1) * P], b.xT[:, k, c, :],
                                                      start=c == 0, stop=c == DC - 1)
                    else:
                        for c in range(DC):
                            mm = nc.tensor.matmul(b.bank[4 + k][0:n_rows, 0:P], b.wrow[:, c, 0:n_rows],
                                                  b.xT[:, k, c, :], start=c == 0, stop=c == DC - 1)
                    mm.then_inc(s["rows"], 1)
                    if kind == "qkv" or prev is None:
                        wait(pe, s["res_out"], tile - 1)
                        if kind == "qkv":
                            for half in range(DC):
                                for c in range(DC):
                                    mm = nc.tensor.matmul(b.bank[6 + k][:, half * P:(half + 1) * P],
                                                          b.wk[:, c, half * P:(half + 1) * P], b.xT[:, k, c, :],
                                                          start=c == 0, stop=c == DC - 1)
                        else:
                            for c in range(DC):
                                mm = nc.tensor.matmul(b.bank[6 + k][:, 0:D], b.xT[:, k, c, :], b.wres[:, c, :],
                                                      start=c == 0, stop=c == DC - 1)
                        mm.then_inc(s["res"], 1)

                def body(i, first, last):
                    for k in range(2):
                        tile = i * 2 + k
                        if fin:
                            pe.wait_ge(s["fin"], (tile + 1) * steps)
                        else:
                            pe.wait_ge(s[f"in{k}"], 16 * (i + 1))
                        if not first:
                            pe.wait_ge(s["xT_sbuf"], (i - 1) * 2 + k + 1)
                        for c in range(DC):
                            mm = nc.tensor.transpose(b.bank[k][:, c * P:(c + 1) * P], b.xs[:, k, c * P:(c + 1) * P],
                                                     b.ident[:])
                        mm.then_inc(s["xT_psum"], 1)
                        if not (first and k == 0):
                            project(tile - 1, 1 - k, i if k == 1 else i - 1,
                                    first and k == 1)
                peeled(pe, BODY, body)
                project(T - 1, 1, BODY - 1, False)


def attention(nc, b, sem, name, layer, pair, make_penalty):
    gat = layer < 2
    qk = layer == 3
    heads = 2 if gat else 1
    upb = 2 * heads
    unitT = BODY * upb
    s = Semaphores(sem, name)
    pen_t = b.pen_dram.rearrange("(t p) j -> t p j", p=P)
    adj_t = b.adj.rearrange("(t p) j -> t p j", p=P)
    o_t = b.o_dram.rearrange("(t p) d -> t p d", p=P)
    ow = 2 * F if gat else D
    SC = N // SCH

    def col(tile, h):
        if isinstance(tile, int):
            return b.col[:, tile:tile + 1, h:h + 1].rearrange("p o h -> p (o h)")
        return b.col[:, bass.ds(tile, 1), h:h + 1].rearrange("p o h -> p (o h)")

    with nc.Block() as block:
        @block.sync
        def _(sp):
            if not qk:
                for hh in range(heads):
                    h = 2 * pair + hh
                    for q in range(2):
                        sp.dma_start(b.brow[:, 2 * q + hh, :],
                                     b.rows_dram[(HEADS if gat else 1) * q + h, :].partition_broadcast(P)).then_inc(s["rows_in"], 16)

            def body(i, first, last):
                for k in range(2):
                    tile = i * 2 + k
                    t = sp.snap(tile) if not isinstance(i, int) else tile
                    if make_penalty:
                        for c in range(GROUPS):
                            n = GROUPS * (2 * i + k) + c
                            tt = t
                            if not (first and n < 2):
                                sp.wait_ge(s["pen_made"], n - 1)
                            sp.dma_start(b.adj_chunk[:, c % 2, :], adj_t[tt, :, c * GW:(c + 1) * GW]).then_inc(s[f"adj_in{c % 2}"], 16)
                    else:
                        if not first:
                            sp.wait_ge(s["y_ready"], ((i - 1) * 2 + k + 1) * heads)
                        sp.dma_start(b.pen[:, k, :], pen_t[t, :, :]).then_inc(s[f"pen_in{k}"], 16)
                    if qk:
                        if not first:
                            sp.wait_ge(s["s_done"], ((i - 1) * 2 + k + 1) * SC)
                        sp.dma_start(b.qT[:, k, :, :], b.q_dram[t, :, :, :]).then_inc(s[f"q_in{k}"], 16)
            peeled(sp, BODY, body)

        @block.gpsimd
        def _(pool):
            def body(i, first, last):
                for k in range(2):
                    tile = i * 2 + k
                    t = pool.snap(tile) if not isinstance(i, int) else tile
                    if make_penalty:
                        pool.wait_ge(s["pen_made"], GROUPS * (tile + 1))
                        pool.dma_start(pen_t[t, :, :], b.pen[:, k, :]).then_inc(s[f"pen_kept{k}"], 16)
                    pool.wait_ge(s["out_ready"], heads * (tile + 1))
                    pool.dma_start(o_t[t, :, pair * ow:(pair + 1) * ow], b.out[:, k, 0:ow]).then_inc(s[f"out_kept{k}"], 16)
            peeled(pool, BODY, body)
            for k in range(2):
                pool.wait_ge(s[f"out_kept{k}"], 16 * BODY)
                if make_penalty:
                    pool.wait_ge(s[f"pen_kept{k}"], 16 * BODY)

        @block.vector
        def _(dve):
            if not qk:
                dve.wait_ge(s["rows_in"], 16 * 2 * heads)

            def recip(u, v):
                dve.wait_ge(s["e_ready"], u + 1)
                wait(dve, s["out_ready"], u - upb + 1)
                if layer == 1:
                    nc.vector.tensor_scalar(b.lone[:, v:v + 1], b.ymin[:, v:v + 1], BIG, 0.0, ALU.mult,
                                            ALU.mult).then_inc(s["lone"], 1)
                    dve.wait_ge(s["lone"], 2 * u + 1)
                    nc.vector.tensor_tensor(b.lone[:, v:v + 1], b.lone[:, v:v + 1], b.den[:, v:v + 1],
                                            ALU.add).then_inc(s["lone"], 1)
                    dve.wait_ge(s["lone"], 2 * u + 2)
                den = b.lone if layer == 1 else b.den
                nc.vector.reciprocal(b.rden[:, v:v + 1], den[:, v:v + 1]).then_inc(s["recip"], 1)

            def body(i, first, last):
                for k in range(2):
                    tile = i * 2 + k
                    for hh in range(heads):
                        v = heads * k + hh
                        u = i * upb + v
                        slot = v % 2
                        Y = b.Y[:, slot, :]
                        wait(dve, s["e_ready"], u - 1)
                        if not qk:
                            nc.vector.scalar_tensor_tensor(Y, b.brow[:, hh, :], col(tile, 2 * pair + hh),
                                                           b.brow[:, 2 + hh, :], ALU.add, ALU.min).then_inc(s["y_raw"], 1)
                        if hh == 0:
                            if make_penalty:
                                dve.wait_ge(s["pen_made"], GROUPS * (tile + 1))
                            else:
                                dve.wait_ge(s[f"pen_in{k}"], 16 * (i + 1))
                            if qk:
                                dg = (b.pen[:, k, bass.ds(tile * P, P)] if not isinstance(tile, int)
                                      else b.pen[:, k, tile * P:(tile + 1) * P])
                                nc.vector.tensor_tensor(dg, dg, b.diag_big[:], ALU.subtract).then_inc(s["diag"], 1)
                                dve.wait_ge(s["diag"], tile + 1)
                        if qk:
                            for c in range(SC):
                                dve.wait_ge(s["s_done"], u * SC + c + 1)
                                dve.sem_inc(b.passed_dve, 1)
                                nc.vector.tensor_tensor_reduce(
                                    b.Y[:, slot, c * SCH:(c + 1) * SCH], b.bank[6 + c % 2][:, :],
                                    b.pen[:, k, c * SCH:(c + 1) * SCH], 1.0, 3e38, ALU.add, ALU.min,
                                    b.ymin8[:, slot * SC + c:slot * SC + c + 1]).then_inc(s["s_read"], 1)
                            dve.wait_ge(s["s_read"], (u + 1) * SC)
                            nc.vector.tensor_reduce(b.ymin[:, v:v + 1], b.ymin8[:, slot * SC:(slot + 1) * SC], AX_X,
                                                    ALU.min).then_inc(s["y_ready"], 1)
                        else:
                            dve.wait_ge(s["y_raw"], u + 1)
                            dve.sem_inc(b.passed_dve, 1)
                            nc.vector.tensor_tensor_reduce(Y, Y, b.pen[:, k, :], 1.0, 3e38, ALU.add, ALU.min,
                                                           b.ymin[:, v:v + 1]).then_inc(s["y_ready"], 1)
                        if not (first and v == 0):
                            recip(u - 1, (v - 1) % upb)
            peeled(dve, BODY, body)
            recip(unitT - 1, upb - 1)

        @block.scalar
        def _(act):
            def penalty(tile, k, c, kept):
                n = GROUPS * tile + c
                act.wait_ge(s[f"adj_in{c % 2}"], 16 * (2 * tile + c // 2 + 1))
                if c == 0:
                    wait(act, s["y_ready"], (tile - 1) * heads)
                    wait(act, s[f"pen_kept{k}"], 16 * kept)
                nc.scalar.activation(b.pen[:, k, c * GW:(c + 1) * GW], b.adj_chunk[:, c % 2, :], ACT.Relu,
                                     bias=b.big_col[:, 0:1], scale=-BIG).then_inc(s["pen_made"], 1)

            def exp(u, v):
                slot = v % 2
                act.wait_ge(s["y_ready"], u + 1)
                wait(act, s["t_done"], GROUPS * (u - 1))
                wait(act, s["recip"], u - upb + 1)
                nc.scalar.activation(b.E[:, slot, :], b.Y[:, slot, :], ACT.Exp, bias=b.ymin[:, v:v + 1], scale=-1.0,
                                     accum_out=b.den[:, v:v + 1]).then_inc(s["e_ready"], 1)

            def take_acc(u, slot):
                act.wait_ge(s["pv_done"], GROUPS * (u + 1))
                wait(act, s["o_done"], u - 1)
                nc.scalar.activation(b.oT[:, slot, :], b.bank[4 + slot][:, 0:P], ACT.Copy).then_inc(s["oT_ready"], 1)

            def normalise(u, v, i):
                k, hh = v // heads, v % heads
                act.wait_ge(s["o_done"] if gat else s["pv_done"], (u + 1) if gat else GROUPS * (u + 1))
                act.wait_ge(s["recip"], u + 1)
                if hh == 0:
                    wait(act, s[f"out_kept{k}"], 16 * i)
                src = b.bank[6 + v % 2][:, 0:F] if gat else b.bank[4 + v % 2][:, 0:D]
                w = F if gat else D
                nc.scalar.activation(b.out[:, k, hh * w:(hh + 1) * w], src, ACT.Copy,
                                     scale=b.rden[:, v:v + 1]).then_inc(s["out_ready"], 1)

            if make_penalty:
                for c in range(GROUPS):
                    penalty(0, 0, c, 0)
            exp(0, 0)

            def body(i, first, last):
                for v in range(upb):
                    u = i * upb + v
                    k, hh = v // heads, v % heads
                    if make_penalty and not (last and k == 1):
                        for c in range(hh * 2, hh * 2 + 2):
                            penalty(i * 2 + k + 1, 1 - k, c, i + k)
                    more = not (last and v == upb - 1)
                    if more and not qk:
                        exp(u + 1, (v + 1) % upb)
                    before = not (first and v == 0)
                    pv, pi = ((v - 1) % upb, i if v > 0 else i - 1)
                    if before and gat:
                        take_acc(u - 1, pv % 2)
                    for g in range(GROUPS):
                        n = u * GROUPS + g
                        act.wait_ge(s["t_done"], n + 1)
                        wait(act, s["pv_done"], n - GROUPS + 1)
                        src = (b.tp[0] if g % 2 == 0 else b.tp[1])
                        nc.scalar.activation(b.PT[:, g, :], src[:, :], ACT.Copy).then_inc(s["pt_ready"], 1)
                        if g == 1 and before:
                            normalise(u - 1, pv, pi)
                    if more and qk:
                        exp(u + 1, (v + 1) % upb)
            peeled(act, BODY, body)
            if gat:
                take_acc(unitT - 1, (upb - 1) % 2)
            normalise(unitT - 1, upb - 1, BODY - 1)

        @block.tensor
        def _(pe):
            def transposes(u, slot, g):
                n = u * GROUPS + g
                if g == 0:
                    pe.wait_ge(s["e_ready"], u + 1)
                wait(pe, s["pt_ready"], n - 1)
                for q in range(GT):
                    j = g * GT + q
                    mm = nc.tensor.transpose(b.tp[g % 2][:, q * P:(q + 1) * P], b.E[:, slot, j * P:(j + 1) * P],
                                             b.ident[:])
                mm.then_inc(s["t_done"], 1)

            def values(u, v, g):
                slot = v % 2
                hh = v % heads
                pe.wait_ge(s["pt_ready"], u * GROUPS + g + 1)
                if g == 0:
                    wait(pe, s["oT_ready"] if gat else s["out_ready"], u - 1)
                for q in range(GT):
                    j = g * GT + q
                    pt = b.PT[:, g, q * P:(q + 1) * P]
                    if gat:
                        half = j % 2
                        h = 2 * pair + hh
                        mm = nc.tensor.matmul(b.bank[4 + slot][half * F:(half + 1) * F, 0:P],
                                              b.V[:, j, h * F:(h + 1) * F], pt, start=j < 2, stop=j >= T - 2)
                    else:
                        mm = nc.tensor.matmul(b.bank[4 + slot][:, 0:D], pt, b.V[:, j, :], start=j == 0, stop=j == T - 1)
                mm.then_inc(s["pv_done"], 1)

            def combine(u, slot):
                pe.wait_ge(s["oT_ready"], u + 1)
                wait(pe, s["out_ready"], u - 1)
                nc.tensor.matmul(b.bank[6 + slot][:, 0:F], b.oT[:, slot, :], b.halves[:], start=True,
                                 stop=True).then_inc(s["o_done"], 1)

            def scores(i, k, c):
                u = i * 2 + k
                if c == 0:
                    pe.wait_ge(s[f"q_in{k}"], 16 * (i + 1))
                wait(pe, s["s_read"], u * SC + c - 1)
                for d in range(DC):
                    mm = nc.tensor.matmul(b.bank[6 + c % 2][:, :], b.qT[:, k, d, :], b.KT[:, d, c * SCH:(c + 1) * SCH],
                                          start=d == 0, stop=d == DC - 1)
                mm.then_inc(s["s_done"], 1)

            if qk:
                for c in range(SC):
                    scores(0, 0, c)

            def body(i, first, last):
                for v in range(upb):
                    u = i * upb + v
                    slot = v % 2
                    before = not (first and v == 0)

                    def next_scores(g):
                        if qk and not (last and v == upb - 1):
                            for c in (2 * g, 2 * g + 1):
                                scores(i + v, (v + 1) % 2, c)
                    transposes(u, slot, 0)
                    next_scores(0)
                    transposes(u, slot, 1)
                    if gat and before:
                        combine(u - 1, (v - 1) % 2)
                    values(u, v, 0)
                    next_scores(1)
                    transposes(u, slot, 2)
                    values(u, v, 1)
                    next_scores(2)
                    transposes(u, slot, 3)
                    values(u, v, 2)
                    next_scores(3)
                    values(u, v, 3)
            peeled(pe, BODY, body)
            if gat:
                combine(unitT - 1, (upb - 1) % 2)


def graph_layers(nc, x, adj, W0, a1, a2, Wr, br, gamma, beta, W1, a, a_row, Wq, Wk, Wv, out):
    with ExitStack() as ctx:
        def sb(name, shape, dt=F32):
            return ctx.enter_context(nc.sbuf_tensor(name, shape, dt))

        taken = []

        def sem(name):
            taken.append(nc.alloc_semaphore(name=name))
            return taken[-1]

        def stage(make, *args):
            make(nc, b, sem, *args)
            nc.clear_and_free_semaphores(taken)
            nc.all_engine_barrier()
            taken.clear()

        def dram(name, shape, dt=F32):
            return nc.dram_tensor(name, shape, dt, kind="Internal").ap()

        b = Buffers()
        b.passed_dve = ctx.enter_context(nc.semaphore("passed_dve"))
        b.passed_pool = ctx.enter_context(nc.semaphore("passed_pool"))
        b.adj = adj
        b.pen_dram = dram("pen_dram", (N, N), BF16)
        b.o_dram = dram("o_dram", (N, D))
        b.res_dram = dram("res_dram", (N, D))
        b.rows_dram = dram("rows_dram", (2 * HEADS, N))
        b.q_dram = dram("q_dram", (T, P, DC, P))
        x1, x2, x3 = (dram(f"x{n}_dram", (N, D)) for n in (1, 2, 3))

        psum = ctx.enter_context(nc.psum_tensor("psum", [P, 8, 512], F32))
        b.bank = [psum[:, k, :] for k in range(8)]
        b.tp = [psum[:, 2 * k:2 * k + 2, :].rearrange("p a n -> p (a n)") for k in range(2)]

        b.ident = sb("ident", [P, P])
        b.halves = sb("halves", [P, F])
        b.diag_big = sb("diag_big", [P, P], BF16)
        b.big_col = sb("big_col", [P, 1])
        b.minus_half = sb("minus_half", [P, 1])
        b.brow = sb("brow", [P, 4, N])
        b.KT = b.brow[:, 0:DC, :]
        b.V = sb("V", [P, T, D])
        b.col = sb("col", [P, T, HEADS])
        b.Y = sb("Y", [P, 2, N])
        b.E = sb("E", [P, 2, N])
        b.pen = sb("pen", [P, 2, N], BF16)
        b.adj_chunk = sb("adj_chunk", [P, 2, GW], I32)
        b.PT = sb("PT", [P, GROUPS, GW])
        b.oT = sb("oT", [P, 2, P])
        b.out = sb("out_tile", [P, 2, D])
        b.qT = sb("qT", [P, 2, DC, P])
        b.ymin = sb("ymin", [P, 4])
        b.ymin8 = sb("ymin8", [P, 2 * N // SCH])
        b.den = sb("den", [P, 4])
        b.rden = sb("rden", [P, 4])
        b.lone = sb("lone", [P, 4])

        free = b.E[:].rearrange("p a n -> p (a n)")
        at = [0]

        def part(*shape):
            size = 1
            for n in shape:
                size *= n
            ap = free[:, at[0]:at[0] + size]
            at[0] += size
            names = " ".join("abcd"[:len(shape)])
            if len(shape) > 1:
                ap = ap.rearrange(f"p ({names}) -> p {names}", **dict(zip("abcd", shape)))
            return ap
        b.xs, b.x_old, b.o_tile, b.res_tile, b.z, b.elu = (part(2, D) for _ in range(6))
        b.xT = part(2, DC, P)
        b.row_tile = part(2, P)
        b.stats = part(2, 6)
        b.mv = part(2, 4)
        b.wx = part(DC, D + HEADS)
        b.wrow = part(DC, 2 * HEADS)
        b.wsum = part(DC, 2, HEADS)
        b.avec = part(2, D)
        b.wprod = part(D)
        b.wres, b.wq, b.wk = (part(DC, D) for _ in range(3))
        b.gamma, b.beta, b.br = (part(D) for _ in range(3))

        stage(constants)
        stage(gat_weights, "g0", W0, a2, a1)
        stage(dense_weights, "g0", [(b.wres, Wr), (b.br, br)])
        stage(tiles_of_rows, "r0", x, None, None, "gat")
        stage(attention, "a00", 0, 0, True)
        stage(attention, "a01", 0, 1, False)
        stage(gat_weights, "g1", W1, a[:, 0:F], a[:, F:2 * F])
        stage(dense_weights, "g1", [(b.gamma, gamma), (b.beta, beta)])
        stage(tiles_of_rows, "r1", x, x1, 0, "gat")
        stage(attention, "a10", 1, 0, False)
        stage(attention, "a11", 1, 1, False)
        stage(row_weights, "g2", a_row)
        stage(tiles_of_rows, "r2", x1, x2, 1, "row")
        stage(attention, "a2", 2, 0, False)
        stage(dense_weights, "g3", [(b.wx[:, :, 0:D], Wv), (b.wq, Wq), (b.wk, Wk)])
        stage(tiles_of_rows, "r3", x2, x3, 2, "qkv")
        stage(attention, "a3", 3, 0, False)
        stage(tiles_of_rows, "r4", x3, out, 3, None)


_INS = ["x", "adj", "L0_gnn_W", "L0_gnn_a1", "L0_gnn_a2", "L0_gnn_Wr", "L0_gnn_br", "L0_gnn_gamma", "L0_gnn_beta",
        "L1_gnn_W", "L1_gnn_a", "L2_gnn_a", "L3_gnn_Wq", "L3_gnn_Wk", "L3_gnn_Wv"]
_OUTS = [((N, D), "float32")]


def kernel(**inputs):
    import numpy as _np
    import concourse.bacc as _bacc
    from concourse import mybir as _mybir
    from concourse.bass_utils import run_bass_kernel_spmd as _run

    nc = _bacc.Bacc("TRN2", target_bir_lowering=False, num_devices=1)
    arrays, args = {}, []
    for name in _INS:
        v = _np.ascontiguousarray(inputs[name])
        arrays[f"in_{name}_dram"] = v
        args.append(nc.dram_tensor(f"in_{name}_dram", v.shape, _mybir.dt.from_np(v.dtype), kind="ExternalInput").ap())
    for i, (shape, dtype) in enumerate(_OUTS):
        dt = _mybir.dt.from_np(_np.dtype(dtype))
        args.append(nc.dram_tensor(f"out_{i}_dram", shape, dt, kind="ExternalOutput").ap())
    graph_layers(nc, *args)
    r = _run(nc, [arrays], core_ids=[0])
    return r.results[0]["out_0_dram"]
```

```python
from contextlib import ExitStack

import concourse.bass as bass
from concourse import mybir

F32 = mybir.dt.float32
BF16 = mybir.dt.bfloat16
I32 = mybir.dt.int32
F32R = mybir.dt.float32r
ALU = mybir.AluOpType
ACT = mybir.ActivationFunctionType
AX_X = mybir.AxisListType.X

P = 128
N = 4096
D = 256
HEADS = 4
F = D // HEADS
T = N // P
DC = D // P
PAIRS = HEADS // 2
BODY = T // 2
GROUPS = 4
GW = N // GROUPS
GT = GW // P
SCH = 512
BIG = 2.0 ** 100
LN_EPS = 1e-5
GAT_SLOPE = 0.2
ROW_SLOPE = 0.01


def wait(eng, sem, count):
    if isinstance(count, int) and count <= 0:
        return
    eng.wait_ge(sem, count)


def peeled(eng, n, body):
    body(0, first=True, last=False)
    with eng.Fori(1, n - 1) as i:
        body(i, first=False, last=False)
    body(n - 1, first=False, last=True)


class Semaphores:

    def __init__(self, sem, name):
        self.sem, self.name, self.made = sem, name, {}

    def __getitem__(self, what):
        if what not in self.made:
            self.made[what] = self.sem(f"{self.name}_{what}")
        return self.made[what]


class Buffers:
    pass


def constants(nc, b, sem):
    made = sem("const_made")
    with nc.Block() as block:
        @block.gpsimd
        def _(pool):
            nc.gpsimd.memset(b.ident[:], 0.0).then_inc(made, 1)
            nc.gpsimd.memset(b.halves[:], 0.0).then_inc(made, 1)
            nc.gpsimd.memset(b.diag_big[:], 0.0).then_inc(made, 1)
            nc.gpsimd.memset(b.big_col[:], BIG).then_inc(made, 1)
            nc.gpsimd.memset(b.minus_half[:], -0.5).then_inc(made, 1)
            pool.wait_ge(made, 5)
            nc.gpsimd.affine_select(out=b.ident[:], in_=b.ident[:], compare_op=ALU.not_equal, fill=1.0, base=0,
                                    pattern=[[-1, P]], channel_multiplier=1).then_inc(made, 1)
            nc.gpsimd.affine_select(out=b.diag_big[:], in_=b.diag_big[:], compare_op=ALU.not_equal, fill=BIG, base=0,
                                    pattern=[[-1, P]], channel_multiplier=1).then_inc(made, 1)
            nc.gpsimd.affine_select(out=b.halves[:], in_=b.halves[:], compare_op=ALU.not_equal, fill=1.0, base=0,
                                    pattern=[[-1, F]], channel_multiplier=1).then_inc(made, 1)
            pool.wait_ge(made, 8)
            nc.gpsimd.affine_select(out=b.halves[:], in_=b.halves[:], compare_op=ALU.not_equal, fill=1.0, base=-F,
                                    pattern=[[-1, F]], channel_multiplier=1).then_inc(made, 1)
            pool.wait_ge(made, 9)


def gat_weights(nc, b, sem, name, W, a_self, a_other):
    loaded, did = sem(f"{name}_w_loaded"), sem(f"{name}_w_did")
    with nc.Block() as block:
        @block.sync
        def _(sp):
            for c in range(DC):
                sp.dma_start(b.wx[:, c, 0:D].rearrange("p (h k) -> p h k", h=HEADS),
                             W[:, c * P:(c + 1) * P, :].rearrange("h p k -> p h k")).then_inc(loaded, 16)
            sp.dma_start(b.avec[:, 0, :].rearrange("p (h k) -> p h k", h=HEADS),
                         a_self.partition_broadcast(P)).then_inc(loaded, 16)
            sp.dma_start(b.avec[:, 1, :].rearrange("p (h k) -> p h k", h=HEADS),
                         a_other.partition_broadcast(P)).then_inc(loaded, 16)

        @block.vector
        def _(dve):
            dve.wait_ge(loaded, 16 * (DC + 2))
            n = 0
            for c in range(DC):
                for s in range(2):
                    if n:
                        dve.wait_ge(did, n)
                    nc.vector.tensor_tensor(b.wprod[:], b.wx[:, c, 0:D], b.avec[:, s, :], ALU.mult).then_inc(did, 1)
                    dve.wait_ge(did, n + 1)
                    nc.vector.tensor_reduce(b.wsum[:, c, s, :], b.wprod[:].rearrange("p (h k) -> p h k", h=HEADS),
                                            AX_X, ALU.add).then_inc(did, 1)
                    n += 2
            dve.wait_ge(did, n)
            for c in range(DC):
                nc.vector.tensor_scalar(b.wx[:, c, D:D + HEADS], b.wsum[:, c, 0, :], -(1 - GAT_SLOPE), None,
                                        ALU.mult).then_inc(did, 1)
                nc.vector.tensor_scalar(b.wrow[:, c, 0:HEADS], b.wsum[:, c, 1, :], -1.0, None,
                                        ALU.mult).then_inc(did, 1)
                nc.vector.tensor_scalar(b.wrow[:, c, HEADS:2 * HEADS], b.wsum[:, c, 1, :], -GAT_SLOPE, None,
                                        ALU.mult).then_inc(did, 1)
            dve.wait_ge(did, n + 3 * DC)


def row_weights(nc, b, sem, name, a):
    loaded, did = sem(f"{name}_w_loaded"), sem(f"{name}_w_did")
    with nc.Block() as block:
        @block.sync
        def _(sp):
            sp.dma_start(b.wsum[:].rearrange("p c s h -> p (c s h)")[:, 0:2 * DC],
                         a.rearrange("(s p) one -> p (s one)", p=P), allow_slow_non_contiguous=True).then_inc(loaded, 16)

        @block.vector
        def _(dve):
            dve.wait_ge(loaded, 16)
            cols = b.wsum[:].rearrange("p c s h -> p (c s h)")
            for c in range(DC):
                nc.vector.tensor_scalar(b.wx[:, c, D:D + 1], cols[:, c:c + 1], -(1 - ROW_SLOPE), None,
                                        ALU.mult).then_inc(did, 1)
                nc.vector.tensor_scalar(b.wrow[:, c, 0:1], cols[:, DC + c:DC + c + 1], -1.0, None,
                                        ALU.mult).then_inc(did, 1)
                nc.vector.tensor_scalar(b.wrow[:, c, 1:2], cols[:, DC + c:DC + c + 1], -ROW_SLOPE, None,
                                        ALU.mult).then_inc(did, 1)
            dve.wait_ge(did, 3 * DC)


def dense_weights(nc, b, sem, name, pairs):
    loaded = sem(f"{name}_dense_loaded")
    with nc.Block() as block:
        @block.sync
        def _(sp):
            for dst, src in pairs:
                if len(src.shape) == 1:
                    sp.dma_start(dst, src.partition_broadcast(P)).then_inc(loaded, 16)
                else:
                    sp.dma_start(dst, src.rearrange("(c p) n -> p c n", p=P)).then_inc(loaded, 16)
            sp.wait_ge(loaded, 16 * len(pairs))


def tiles_of_rows(nc, b, sem, name, x_in, x_out, prev, kind):
    s = Semaphores(sem, name)
    fin = prev is not None
    elu = prev == 0
    n_rows = {"gat": 2 * HEADS, "row": 2}.get(kind, 0)
    n_in = 1 + fin + elu
    xin = x_in.rearrange("(g k p) d -> g p k d", p=P, k=2)
    o_in = b.o_dram.rearrange("(g k p) d -> g p k d", p=P, k=2)
    res_in = b.res_dram.rearrange("(g k p) d -> g p k d", p=P, k=2)
    xo = None if x_out is None else x_out.rearrange("(g k p) d -> g p k d", p=P, k=2)
    rows_out = b.rows_dram.rearrange("r (g n) -> g r n", n=2 * P)

    def groups(eng, lags, step):
        most = max(lag for _, lag in lags)

        def turn(t, slot, i):
            for what, lag in lags:
                g = t - lag
                if isinstance(t, int) and not 0 <= g < BODY:
                    continue
                step(what, g, (slot - lag) % 2, i - (lag - slot + 1) // 2)
        lead = most + 2 + most % 2
        for t in range(lead):
            turn(t, t % 2, t // 2)
        with eng.Fori(lead // 2, BODY // 2) as i:
            turn(i * 2, 0, i)
            turn(i * 2 + 1, 1, i)
        for t in range(BODY, BODY + most):
            turn(t, t % 2, t // 2)

    def at(g, buf, size=1, *rest):
        if isinstance(g, int):
            return buf[(slice(None), slice(size * g, size * (g + 1))) + rest]
        return buf[(slice(None), bass.ds(g * size, size)) + rest]

    def transposed(n):
        return s["xT_bank"], DC * n

    def projected(n):
        if prev is None:
            return s["res"], 2 * n
        return s["rows"], (DC if kind == "qkv" else 1) * n

    with nc.Block() as block:
        @block.sync
        def _(sp):
            def step(what, g, slot, i):
                gg = g if isinstance(g, int) else sp.snap(g)
                wait(sp, *((s["new"], g - 1) if fin else transposed(g - 1)))
                sp.dma_start((b.x_old if fin else b.xs)[:, slot, :, :], xin[gg, :, :, :]).then_inc(s[f"in{slot}"], 16)
                if fin:
                    sp.dma_start(b.o_tile[:, slot, :, :], o_in[gg, :, :, :]).then_inc(s[f"in{slot}"], 16)
                if elu:
                    sp.dma_start(b.res_tile[:, slot, :, :], res_in[gg, :, :, :]).then_inc(s[f"in{slot}"], 16)
            groups(sp, [("load", 0)], step)

        @block.vector
        def _(dve):
            def step(what, g, slot, i):
                o = b.o_tile[:, slot, :, :]
                if what == "sum":
                    dve.wait_ge(s[f"in{slot}"], 16 * n_in * (i + 1))
                    if elu:
                        dve.wait_ge(s["exp"], g + 1)
                        nc.vector.scalar_tensor_tensor(o, o, 0.0, b.elu[:, slot, :, :], ALU.max,
                                                       ALU.add).then_inc(s["elu_sum"], 1)
                        dve.wait_ge(s["elu_sum"], g + 1)
                        nc.vector.scalar_tensor_tensor(o, o, -1.0, b.res_tile[:, slot, :, :], ALU.add,
                                                       ALU.add).then_inc(s["sum"], 1)
                    else:
                        nc.vector.tensor_tensor(o, o, b.x_old[:, slot, :, :], ALU.add).then_inc(s["sum"], 1)
                    dve.wait_ge(s["sum"], g + 1)
                    for k in range(2):
                        nc.vector.bn_stats(b.stats[:, slot, k, :], o[:, k, :]).then_inc(s["stats"], 1)
                    dve.wait_ge(s["stats"], 2 * g + 2)
                    dve.sem_inc(b.passed_dve, 1)
                    for k in range(2):
                        nc.vector.bn_aggr(b.mv[:, slot, k, 0:2], b.stats[:, slot, k, :]).then_inc(s["moments"], 1)
                if what == "norm1":
                    dve.wait_ge(s["rstd"], 2 * (g + 1))
                    for k in range(2):
                        nc.vector.tensor_scalar(o[:, k, :], o[:, k, :], b.mv[:, slot, k, 0:1], b.mv[:, slot, k, 3:4],
                                                ALU.subtract, ALU.mult).then_inc(s["norm1"], 1)
                if what == "sum2":
                    dve.wait_ge(s["affine"], g + 1)
                    for k in range(2):
                        nc.vector.bn_stats(b.stats[:, slot, k, :], o[:, k, :]).then_inc(s["stats2"], 1)
                    dve.wait_ge(s["stats2"], 2 * g + 2)
                    dve.sem_inc(b.passed_dve, 1)
                    for k in range(2):
                        nc.vector.bn_aggr(b.mv[:, slot, k, 0:2], b.stats[:, slot, k, :]).then_inc(s["moments2"], 1)
                if what == "new":
                    dve.wait_ge(s["rstd2" if elu else "rstd"], 2 * (g + 1))
                    wait(dve, s[f"x_kept{slot}"], 16 * i)
                    if kind is not None:
                        wait(dve, *transposed(g - 1))
                    if kind == "row":
                        wait(dve, s["v_low"], g - 1)
                    for k in range(2):
                        ins = nc.vector.tensor_scalar(b.xs[:, slot, k, :], o[:, k, :], b.mv[:, slot, k, 0:1],
                                                      b.mv[:, slot, k, 3:4], ALU.subtract, ALU.mult)
                    ins.then_inc(s["new"], 1)
                if what == "take":
                    for k in range(2):
                        tile = 2 * g + k
                        dve.wait_ge(s["proj"], tile + 1)
                        if kind == "row":
                            nc.vector.tensor_copy(at(tile, b.col, 1, slice(0, 1)),
                                                  b.bank[2 + k][:, D:D + 1].rearrange("p (o n) -> p o n", o=1)).then_inc(s["proj_out"], 1)
                            continue
                        v_psum = b.bank[2 + k][:, 0:D].rearrange("p (o n) -> p o n", o=1)
                        if kind == "gat":
                            nc.vector.tensor_copy(at(tile, b.col, 1, slice(None)),
                                                  b.bank[2 + k][:, D:D + HEADS].rearrange("p (o n) -> p o n", o=1))
                            nc.vector.tensor_copy(at(tile, b.V, 1, slice(None)), v_psum).then_inc(s["proj_out"], 1)
                        if kind == "qkv":
                            dve.wait_ge(s["v_high"], tile + 1)
                            nc.vector.tensor_tensor(at(tile, b.V2, 1, 1, slice(None)), v_psum,
                                                    at(tile, b.V2, 1, 0, slice(None)).bitcast(F32),
                                                    ALU.subtract).then_inc(s["proj_out"], 1)
                    if kind == "qkv":
                        for c in range(DC):
                            dve.wait_ge(s["k_high"], DC * g + c + 1)
                            cols = slice(2 * P * g, 2 * P * (g + 1)) if isinstance(g, int) else bass.ds(g * 2 * P, 2 * P)
                            nc.vector.tensor_tensor(b.KT2[:, 1, c, cols], b.bank[6 + c][:, 0:2 * P],
                                                    b.KT2[:, 0, c, cols].bitcast(F32),
                                                    ALU.subtract).then_inc(s["k_low"], 1)
                            dve.wait_ge(s["q_high"], DC * g + c + 1)
                            if c == 0:
                                wait(dve, s[f"rows_kept{slot}"], 16 * i)
                            nc.vector.scalar_tensor_tensor(b.q_stage[:, slot, 1, c, :], b.bank[4 + c][:, 0:2 * P], -1.0,
                                                           b.q_stage[:, slot, 0, c, :].bitcast(F32), ALU.mult,
                                                           ALU.subtract).then_inc(s["q_low"], 1)
                    if prev is None:
                        wait(dve, s[f"res_kept{slot}"], 16 * i)
                        for k in range(2):
                            dve.wait_ge(s["res"], 2 * g + k + 1)
                            nc.vector.tensor_tensor(b.res_tile[:, slot, k, :], b.bank[6 + k][:, 0:D], b.br[:],
                                                    ALU.add).then_inc(s["res_out"], 1)
            if elu:
                lags = [("sum", 0), ("sum2", 1), ("norm1", 0), ("new", 1), ("take", 3)]
            elif fin:
                lags = [("sum", 0), ("new", 1)] + [("take", 3)] * (kind is not None)
            else:
                lags = [("take", 2)]
            groups(dve, lags, step)

        @block.gpsimd
        def _(pool):
            def rstd(g, slot, measured, eps, done):
                pool.wait_ge(measured, 2 * (g + 1))
                pool.sem_inc(b.passed_pool, 1)
                nc.gpsimd.tensor_scalar(b.mv[:, slot, :, 2:3], b.mv[:, slot, :, 1:2], LN_EPS, None,
                                        ALU.add).then_inc(eps, 1)
                pool.wait_ge(eps, g + 1)
                for k in range(2):
                    nc.gpsimd.tensor_tensor(b.mv[:, slot, k, 3:4], b.mv[:, slot, k, 2:3], b.minus_half[:],
                                            ALU.pow).then_inc(done, 1)

            def step(what, g, slot, i):
                o = b.o_tile[:, slot, :, :]
                if what == "rstd":
                    rstd(g, slot, s["moments"], s["eps"], s["rstd"])
                if what == "rstd2":
                    rstd(g, slot, s["moments2"], s["eps2"], s["rstd2"])
                if what == "affine":
                    pool.wait_ge(s["norm1"], 2 * (g + 1))
                    for n, other in enumerate((b.gamma2, b.beta2, b.x_old[:, slot, :, :])):
                        if n:
                            pool.wait_ge(s["part"], 2 * g + n)
                        nc.gpsimd.tensor_tensor(o, o, other, ALU.add if n else ALU.mult).then_inc(
                            s["part"] if n < 2 else s["affine"], 1)
                if what == "v_low":
                    pool.wait_ge(s["v_high"], g + 1)
                    nc.gpsimd.tensor_tensor(at(g, b.V2, 2, 1, slice(None)), b.xs[:, slot, :, :],
                                            at(g, b.V2, 2, 0, slice(None)).bitcast(F32),
                                            ALU.subtract).then_inc(s["v_low"], 1)
            if elu:
                groups(pool, [("rstd", 0), ("rstd2", 1), ("affine", 0)], step)
            elif fin:
                groups(pool, [("rstd", 0)] + [("v_low", 2)] * (kind == "row"), step)

        @block.scalar
        def _(act):
            def step(what, g, slot, i):
                gg = g if isinstance(g, int) else act.snap(g)
                if what == "exp":
                    act.wait_ge(s[f"in{slot}"], 16 * n_in * (i + 1))
                    wait(act, s["elu_sum"], g - 1)
                    nc.scalar.activation(b.elu[:, slot, :, :], b.o_tile[:, slot, :, :], ACT.Relu,
                                         scale=-1.0).then_inc(s["relu"], 1)
                    act.wait_ge(s["relu"], g + 1)
                    nc.scalar.activation(b.elu[:, slot, :, :], b.elu[:, slot, :, :], ACT.Exp,
                                         scale=-1.0).then_inc(s["exp"], 1)
                if what == "keep":
                    act.wait_ge(s["new"], g + 1)
                    act.dma_start(xo[gg, :, :, :], b.xs[:, slot, :, :]).then_inc(s[f"x_kept{slot}"], 16)
                if what == "xT":
                    for c in range(DC):
                        act.wait_ge(s["xT_bank"], DC * g + c + 1)
                        if c == 0:
                            wait(act, *projected(g - 1))
                        ins = nc.scalar.activation(b.xT[:, slot, c, :], b.bank[c][:, 0:2 * P], ACT.Copy)
                        ins.then_inc(s["xT_sbuf"], 1)
                    if kind == "row":
                        nc.scalar.activation(at(g, b.V2, 2, 0, slice(None)), b.xs[:, slot, :, :],
                                             ACT.Copy).then_inc(s["v_high"], 1)
                if what == "take":
                    if kind == "qkv":
                        for k in range(2):
                            act.wait_ge(s["proj"], 2 * g + k + 1)
                            nc.scalar.activation(at(2 * g + k, b.V2, 1, 0, slice(None)),
                                                 b.bank[2 + k][:, 0:D].rearrange("p (o n) -> p o n", o=1),
                                                 ACT.Copy).then_inc(s["v_high"], 1)
                        for c in range(DC):
                            cols = slice(2 * P * g, 2 * P * (g + 1)) if isinstance(g, int) else bass.ds(g * 2 * P, 2 * P)
                            act.wait_ge(s["keys"], DC * g + c + 1)
                            nc.scalar.activation(b.KT2[:, 0, c, cols], b.bank[6 + c][:, 0:2 * P],
                                                 ACT.Copy).then_inc(s["k_high"], 1)
                            act.wait_ge(s["rows"], DC * g + c + 1)
                            if c == 0:
                                wait(act, s[f"rows_kept{slot}"], 16 * i)
                            nc.scalar.activation(b.q_stage[:, slot, 0, c, :], b.bank[4 + c][:, 0:2 * P], ACT.Copy,
                                                 scale=-1.0).then_inc(s["q_high"], 1)
                        act.wait_ge(s["q_low"], DC * (g + 1))
                        act.dma_start(b.q_dram[gg, :, :, :, :], b.q_stage[:, slot, :, :, :].bitcast(F32)).then_inc(s[f"rows_kept{slot}"], 16)
                    else:
                        act.wait_ge(s["rows"], g + 1)
                        wait(act, s[f"rows_kept{slot}"], 16 * i)
                        nc.scalar.activation(b.row_tile[0:n_rows, slot, :], b.bank[4 + slot][0:n_rows, 0:2 * P],
                                             ACT.Copy).then_inc(s["rows_out"], 1)
                        act.wait_ge(s["rows_out"], g + 1)
                        act.dma_start(rows_out[gg, 0:n_rows, :], b.row_tile[0:n_rows, slot, :]).then_inc(s[f"rows_kept{slot}"], 16)
                if what == "keep_res":
                    act.wait_ge(s["res_out"], 2 * (g + 1))
                    act.dma_start(res_in[gg, :, :, :], b.res_tile[:, slot, :, :]).then_inc(s[f"res_kept{slot}"], 16)
            lags = [("exp", 0)] * elu + [("keep", 1)] * fin
            if kind is not None:
                lags += [("xT", 1 + fin), ("take", 2 + fin)]
            if prev is None:
                lags += [("keep_res", 2)]
            groups(act, lags, step)
            for slot in range(2):
                if fin:
                    act.wait_ge(s[f"x_kept{slot}"], 16 * BODY // 2)
                if kind is not None:
                    act.wait_ge(s[f"rows_kept{slot}"], 16 * BODY // 2)
                if prev is None:
                    act.wait_ge(s[f"res_kept{slot}"], 16 * BODY // 2)

        if kind is not None:
            @block.tensor
            def _(pe):
                def step(what, g, slot, i):
                    if what == "xT":
                        if fin:
                            pe.wait_ge(s["new"], g + 1)
                        else:
                            pe.wait_ge(s[f"in{slot}"], 16 * (i + 1))
                        for c in range(DC):
                            wait(pe, s["xT_sbuf"], DC * (g - 1) + c + 1)
                            for k in range(2):
                                mm = nc.tensor.transpose(b.bank[c][:, k * P:(k + 1) * P],
                                                         b.xs[:, slot, k, c * P:(c + 1) * P], b.ident[:])
                            mm.then_inc(s["xT_bank"], 1)
                    if what == "project":
                        pe.wait_ge(s["xT_sbuf"], DC * (g + 1))
                        a, z = {"gat": (0, D + HEADS), "row": (D, D + 1), "qkv": (0, D)}[kind]
                        for k in range(2):
                            wait(pe, s["proj_out"], 2 * (g - 1) + k + 1)
                            for c in range(DC):
                                mm = nc.tensor.matmul(b.bank[2 + k][:, a:z], b.xT[:, slot, c, k * P:(k + 1) * P],
                                                      b.wx[:, c, a:z], start=c == 0, stop=c == DC - 1)
                            mm.then_inc(s["proj"], 1)
                        if kind == "qkv":
                            for w, bank, made, taken in ((b.wk, 6, "keys", "k_low"), (b.wq, 4, "rows", "q_low")):
                                for half in range(DC):
                                    wait(pe, s[taken], DC * (g - 1) + half + 1)
                                    for c in range(DC):
                                        mm = nc.tensor.matmul(b.bank[bank + half][:, 0:2 * P],
                                                              w[:, c, half * P:(half + 1) * P], b.xT[:, slot, c, :],
                                                              start=c == 0, stop=c == DC - 1)
                                    mm.then_inc(s[made], 1)
                        else:
                            wait(pe, s["rows_out"], g - 1)
                            for c in range(DC):
                                mm = nc.tensor.matmul(b.bank[4 + slot][0:n_rows, 0:2 * P], b.wrow[:, c, 0:n_rows],
                                                      b.xT[:, slot, c, :], start=c == 0, stop=c == DC - 1)
                            mm.then_inc(s["rows"], 1)
                        if prev is None:
                            for k in range(2):
                                wait(pe, s["res_out"], 2 * (g - 1) + k + 1)
                                for c in range(DC):
                                    mm = nc.tensor.matmul(b.bank[6 + k][:, 0:D], b.xT[:, slot, c, k * P:(k + 1) * P],
                                                          b.wres[:, c, :], start=c == 0, stop=c == DC - 1)
                                mm.then_inc(s["res"], 1)
                groups(pe, [("xT", 0 + fin), ("project", 1 + fin)], step)


def column(b, tile, h):
    if isinstance(tile, int):
        return b.col[:, tile:tile + 1, h:h + 1].rearrange("p o h -> p (o h)")
    return b.col[:, bass.ds(tile, 1), h:h + 1].rearrange("p o h -> p (o h)")


def gat_attention(nc, b, sem, name, layer, pair, make_penalty):
    s = Semaphores(sem, name)
    pen_t = b.pen_dram.rearrange("(t p) j -> t p j", p=P)
    adj_t = b.adj.rearrange("(t p) j -> t p j", p=P)
    o_t = b.o_dram.rearrange("(t p) d -> t p d", p=P)
    UNITS = 4
    ALL = BODY * UNITS

    with nc.Block() as block:
        @block.sync
        def _(sp):
            def load_rows(hh):
                for q in range(2):
                    sp.dma_start(b.brow[:, 2 * q + hh, :],
                                 b.rows_dram[HEADS * q + 2 * pair + hh, :].partition_broadcast(P)).then_inc(s[f"rows_in{hh}"], 16)

            load_rows(0)

            def body(i, first, last):
                for k in range(2):
                    tile = i * 2 + k
                    t = tile if isinstance(i, int) else sp.snap(tile)
                    if make_penalty:
                        for c in range(GROUPS):
                            wait(sp, s["pen_made"], GROUPS * tile + c - 1)
                            sp.dma_start(b.adj_chunk[:, c % 2, :], adj_t[t, :, c * GW:(c + 1) * GW]).then_inc(s[f"adj_in{c % 2}"], 16)
                    else:
                        wait(sp, s["y_ready"], (tile - 1) * 2)
                        sp.dma_start(b.pen[:, k, :], pen_t[t, :, :]).then_inc(s[f"pen_in{k}"], 16)
                    if first and k == 0:
                        load_rows(1)
            peeled(sp, BODY, body)

        @block.gpsimd
        def _(pool):
            def lone(u, v):
                pool.wait_ge(s["e_ready"], u + 1)
                wait(pool, s["recip"], u - UNITS + 1)
                pool.sem_inc(b.passed_pool, 1)
                nc.gpsimd.tensor_scalar(b.lone[:, v:v + 1], b.ymin[:, v:v + 1], BIG, 0.0, ALU.mult,
                                        ALU.mult).then_inc(s["lone"], 1)
                pool.wait_ge(s["lone"], u + 1)
                nc.gpsimd.tensor_tensor(b.sums[:, v:v + 1], b.lone[:, v:v + 1], b.den[:, v:v + 1],
                                        ALU.add).then_inc(s["sums"], 1)

            def body(i, first, last):
                for k in range(2):
                    tile = i * 2 + k
                    t = tile if isinstance(i, int) else pool.snap(tile)
                    if make_penalty:
                        pool.wait_ge(s["pen_made"], GROUPS * (tile + 1))
                        pool.dma_start(pen_t[t, :, :], b.pen[:, k, :]).then_inc(s[f"pen_kept{k}"], 16)
                    if layer == 1:
                        for hh in range(2):
                            lone(i * UNITS + 2 * k + hh, 2 * k + hh)
                    if not (first and k == 0):
                        keep(i if k == 1 else i - 1, 1 - k)

            def keep(i, k):
                tile = i * 2 + k
                t = tile if isinstance(i, int) else pool.snap(tile)
                pool.wait_ge(s["out_ready"], 2 * (tile + 1))
                pool.dma_start(o_t[t, :, pair * 2 * F:(pair + 1) * 2 * F], b.out[:, k, 0:2 * F]).then_inc(s[f"out_kept{k}"], 16)
            peeled(pool, BODY, body)
            keep(BODY - 1, 1)
            for k in range(2):
                pool.wait_ge(s[f"out_kept{k}"], 16 * BODY)
                if make_penalty:
                    pool.wait_ge(s[f"pen_kept{k}"], 16 * BODY)

        @block.vector
        def _(dve):
            def recip(u, v):
                dve.wait_ge(s["sums" if layer == 1 else "e_ready"], u + 1)
                wait(dve, s["out_ready"], u - UNITS + 1)
                sums = b.sums if layer == 1 else b.den
                nc.vector.reciprocal(b.rden[:, v:v + 1], sums[:, v:v + 1]).then_inc(s["recip"], 1)

            def body(i, first, last):
                for v in range(UNITS):
                    u = i * UNITS + v
                    k, hh = v // 2, v % 2
                    tile = i * 2 + k
                    Y = b.Y[:, v % 2, :]
                    if first and k == 0:
                        dve.wait_ge(s[f"rows_in{hh}"], 16 * 2)
                    wait(dve, s["e_ready"], u - 1)
                    nc.vector.scalar_tensor_tensor(Y, b.brow[:, hh, :], column(b, tile, 2 * pair + hh),
                                                   b.brow[:, 2 + hh, :], ALU.add, ALU.min).then_inc(s["y_raw"], 1)
                    if hh == 0:
                        if make_penalty:
                            dve.wait_ge(s["pen_made"], GROUPS * (tile + 1))
                        else:
                            dve.wait_ge(s[f"pen_in{k}"], 16 * (i + 1))
                    if layer == 1:
                        wait(dve, s["lone"], u - UNITS + 1)
                    dve.wait_ge(s["y_raw"], u + 1)
                    dve.sem_inc(b.passed_dve, 1)
                    nc.vector.tensor_tensor_reduce(Y, Y, b.pen[:, k, :], 1.0, 3e38, ALU.add, ALU.min,
                                                   b.ymin[:, v:v + 1]).then_inc(s["y_ready"], 1)
                    if not (first and v == 0):
                        recip(u - 1, (v - 1) % UNITS)
            peeled(dve, BODY, body)
            recip(ALL - 1, UNITS - 1)

        @block.scalar
        def _(act):
            def penalty(tile, k, c, kept):
                act.wait_ge(s[f"adj_in{c % 2}"], 16 * (2 * tile + c // 2 + 1))
                if c == 0:
                    wait(act, s["y_ready"], (tile - 1) * 2)
                    wait(act, s[f"pen_kept{k}"], 16 * kept)
                nc.scalar.activation(b.pen[:, k, c * GW:(c + 1) * GW], b.adj_chunk[:, c % 2, :], ACT.Relu,
                                     bias=b.big_col[:, 0:1], scale=-BIG).then_inc(s["pen_made"], 1)

            def exp(u, v):
                act.wait_ge(s["y_ready"], u + 1)
                wait(act, s["t_done"], GROUPS * (u - 1))
                wait(act, s["recip"], u - UNITS + 1)
                nc.scalar.activation(b.E[:, v % 2, :], b.Y[:, v % 2, :], ACT.Exp, bias=b.ymin[:, v:v + 1], scale=-1.0,
                                     accum_out=b.den[:, v:v + 1]).then_inc(s["e_ready"], 1)

            def take_acc(u, slot):
                act.wait_ge(s["pv_done"], GROUPS * (u + 1))
                wait(act, s["o_done"], u - 1)
                nc.scalar.activation(b.oT[:, slot, :], b.bank[4 + slot][:, 0:P], ACT.Copy).then_inc(s["oT_ready"], 1)

            def normalise(u, v, i):
                k, hh = v // 2, v % 2
                act.wait_ge(s["o_done"], u + 1)
                act.wait_ge(s["recip"], u + 1)
                if hh == 0:
                    wait(act, s[f"out_kept{k}"], 16 * i)
                nc.scalar.activation(b.out[:, k, hh * F:(hh + 1) * F], b.bank[6 + v % 2][:, 0:F], ACT.Copy,
                                     scale=b.rden[:, v:v + 1]).then_inc(s["out_ready"], 1)

            if make_penalty:
                for c in range(GROUPS):
                    penalty(0, 0, c, 0)
                for c in range(GROUPS // 2):
                    penalty(1, 1, c, 0)
            exp(0, 0)

            def body(i, first, last):
                for v in range(UNITS):
                    u = i * UNITS + v
                    k, hh = v // 2, v % 2
                    before = not (first and v == 0)
                    if make_penalty and hh == 0 and not (last and k == 1):
                        for c in range(GROUPS // 2, GROUPS):
                            penalty(i * 2 + k + 1, 1 - k, c, i + k)
                    if not (last and v == UNITS - 1):
                        exp(u + 1, (v + 1) % UNITS)
                    if make_penalty and hh == 1 and not last:
                        for c in range(GROUPS // 2):
                            penalty(i * 2 + k + 2, k, c, i + 1)
                    if before:
                        take_acc(u - 1, (v - 1) % 2)
                    for g in range(GROUPS):
                        n = u * GROUPS + g
                        act.wait_ge(s["t_done"], n + 1)
                        wait(act, s["pv_done"], n - GROUPS + 1)
                        nc.scalar.activation(b.PT[:, g, :], b.tp[g % 2][:, :], ACT.Copy).then_inc(s["pt_ready"], 1)
                        if g == 1 and before:
                            normalise(u - 1, (v - 1) % UNITS, i if v > 0 else i - 1)
            peeled(act, BODY, body)
            take_acc(ALL - 1, 1)
            normalise(ALL - 1, UNITS - 1, BODY - 1)

        @block.tensor
        def _(pe):
            def transposes(u, slot, g):
                n = u * GROUPS + g
                if g == 0:
                    pe.wait_ge(s["e_ready"], u + 1)
                wait(pe, s["pt_ready"], n - 1)
                for q in range(GT):
                    j = g * GT + q
                    mm = nc.tensor.transpose(b.tp[g % 2][:, q * P:(q + 1) * P], b.E[:, slot, j * P:(j + 1) * P],
                                             b.ident[:])
                mm.then_inc(s["t_done"], 1)

            def values(u, v, g):
                pe.wait_ge(s["pt_ready"], u * GROUPS + g + 1)
                if g == 0:
                    wait(pe, s["oT_ready"], u - 1)
                h = 2 * pair + v % 2
                for q in range(GT):
                    j = g * GT + q
                    half = j % 2
                    mm = nc.tensor.matmul(b.bank[4 + v % 2][half * F:(half + 1) * F, 0:P],
                                          b.V[:, j, h * F:(h + 1) * F], b.PT[:, g, q * P:(q + 1) * P],
                                          start=j < 2, stop=j >= T - 2)
                mm.then_inc(s["pv_done"], 1)

            def combine(u, slot):
                pe.wait_ge(s["oT_ready"], u + 1)
                wait(pe, s["out_ready"], u - 1)
                nc.tensor.matmul(b.bank[6 + slot][:, 0:F], b.oT[:, slot, :], b.halves[:], start=True,
                                 stop=True).then_inc(s["o_done"], 1)

            def body(i, first, last):
                for v in range(UNITS):
                    u = i * UNITS + v
                    transposes(u, v % 2, 0)
                    transposes(u, v % 2, 1)
                    if not (first and v == 0):
                        combine(u - 1, (v - 1) % 2)
                    transposes(u, v % 2, 2)
                    transposes(u, v % 2, 3)
                    for g in range(GROUPS):
                        values(u, v, g)
            peeled(pe, BODY, body)
            combine(ALL - 1, 1)


def row_attention(nc, b, sem, name, layer):
    qk = layer == 3
    s = Semaphores(sem, name)
    pen_t = b.pen_dram.rearrange("(t p) j -> t p j", p=P)
    o_t = b.o_dram.rearrange("(t p) d -> t p d", p=P)
    SPG = GW // SCH
    EXPS = 1 if qk else 2
    X = b.Y if qk else b.E

    with nc.Block() as block:
        @block.sync
        def _(sp):
            if not qk:
                for g in range(GROUPS):
                    for r in range(2):
                        cols = slice(g * GW, (g + 1) * GW)
                        sp.dma_start(b.brow[:, r, cols], b.rows_dram[r, cols].partition_broadcast(P)).then_inc(s[f"rows_in{g}"], 16)

            def body(i, first, last):
                for k in range(2):
                    tile = i * 2 + k
                    t = sp.snap(tile) if not isinstance(i, int) else tile
                    wait(sp, s["y_ready"], tile - 1)
                    sp.dma_start(b.pen[:, k, :], pen_t[t, :, :]).then_inc(s[f"pen_in{k}"], 16)
                    if qk:
                        ii = sp.snap(i) if not isinstance(i, int) else i
                        wait(sp, s["s_done"], (tile - 1) * GROUPS * SPG)
                        sp.dma_start(b.qT2[:, k, :, :, :].bitcast(F32), b.q_dram[ii, :, :, :, k * P:(k + 1) * P]).then_inc(s[f"q_in{k}"], 16)
            peeled(sp, BODY, body)

        @block.gpsimd
        def _(pool):
            def body(i, first, last):
                for k in range(2):
                    tile = i * 2 + k
                    t = pool.snap(tile) if not isinstance(i, int) else tile
                    if not qk:
                        pool.wait_ge(s["e_ready"], 2 * (tile + 1))
                        wait(pool, s["recip"], tile - 1)
                        nc.gpsimd.tensor_tensor(b.sums[:, k:k + 1], b.den[:, 2 * k:2 * k + 1],
                                                b.den[:, 2 * k + 1:2 * k + 2], ALU.add).then_inc(s["sums"], 1)
                        if first and k == 0:
                            continue
                        t = tile - 1 if isinstance(i, int) else pool.snap(tile - 1)
                        keep(tile - 1, t, 1 - k)
                    else:
                        keep(tile, t, k)
            def keep(tile, t, k):
                    pool.wait_ge(s["out_ready"], tile + 1)
                    pool.dma_start(o_t[t, :, :], b.out[:, k, :]).then_inc(s[f"out_kept{k}"], 16)
            peeled(pool, BODY, body)
            if not qk:
                keep(T - 1, T - 1, 1)
            for k in range(2):
                pool.wait_ge(s[f"out_kept{k}"], 16 * BODY)

        @block.vector
        def _(dve):
            def part(i, k, g):
                u = i * 2 + k
                if g == 0:
                    wait(dve, *((s["t_done"], GROUPS * (u - 1)) if qk else (s["e_ready"], EXPS * (u - 1))))
                    dve.wait_ge(s[f"pen_in{k}"], 16 * (i + 1))
                    if qk:
                        dg = b.pen[:, k, u * P:(u + 1) * P] if isinstance(u, int) else b.pen[:, k, bass.ds(u * P, P)]
                        nc.vector.tensor_tensor(dg, dg, b.diag_big[:], ALU.subtract).then_inc(s["diag"], 1)
                        dve.wait_ge(s["diag"], u + 1)
                parts = SPG if qk else 1
                if not qk:
                    cols = slice(g * GW, (g + 1) * GW)
                    nc.vector.scalar_tensor_tensor(b.Y[:, k, cols], b.brow[:, 0, cols], column(b, u, 0),
                                                   b.brow[:, 1, cols], ALU.add, ALU.min).then_inc(s["y_raw"], 1)
                for c in range(parts):
                    n = parts * g + c
                    w = GW // parts
                    cols = slice(n * w, (n + 1) * w)
                    if qk:
                        dve.wait_ge(s["s_done"], u * GROUPS * SPG + n + 1)
                    else:
                        dve.wait_ge(s["y_raw"], u * GROUPS + g + 1)
                    dve.sem_inc(b.passed_dve, 1)
                    nc.vector.tensor_tensor_reduce(b.Y[:, k, cols], b.bank[6 + n % 2][:, :] if qk else b.Y[:, k, cols],
                                                   b.pen[:, k, cols], 1.0, 3e38, ALU.add, ALU.min,
                                                   b.ymin8[:, k, n:n + 1]).then_inc(s["part"], 1)
                if g == GROUPS - 1:
                    dve.wait_ge(s["part"], (u + 1) * GROUPS * parts)
                    nc.vector.tensor_reduce(b.ymin[:, k:k + 1], b.ymin8[:, k, 0:GROUPS * parts], AX_X,
                                            ALU.min).then_inc(s["y_ready"], 1)

            def low(u, g):
                n = u * GROUPS + g
                dve.wait_ge(s["h_ready"], n + 1)
                wait(dve, s["pv_done"], n - 1)
                nc.vector.tensor_tensor(b.PL[:, g % 2, :], b.tp[g % 2][:, :], b.PH[:, g % 2, :].bitcast(F32),
                                        ALU.subtract).then_inc(s["l_ready"], 1)

            def recip(u, k):
                if qk:
                    dve.wait_ge(s["e_ready"], u + 1)
                else:
                    dve.wait_ge(s["sums"], u + 1)
                sums = b.den if qk else b.sums
                nc.vector.reciprocal(b.rden[:, k:k + 1], sums[:, k:k + 1]).then_inc(s["recip"], 1)

            def add_low(u, k):
                dve.wait_ge(s["half_out"], u + 1)
                nc.vector.scalar_tensor_tensor(b.out[:, k, :], b.bank[4 + k][:, D:2 * D], b.rden[:, k:k + 1],
                                               b.out[:, k, :], ALU.mult, ALU.add).then_inc(s["out_ready"], 1)

            def part_after(i, k, g, last):
                if qk:
                    if not (last and k == 1):
                        part(i + k, 1 - k, g)
                elif g == 0:
                    if not (last and k == 1):
                        part(i + k, 1 - k, GROUPS - 1)
                elif not last:
                    part(i + 1, k, g - 1)

            for g in range(GROUPS):
                if not qk:
                    dve.wait_ge(s[f"rows_in{g}"], 16 * 2)
                part(0, 0, g)
            if not qk:
                for g in range(GROUPS - 1):
                    part(0, 1, g)

            def body(i, first, last):
                for k in range(2):
                    u = i * 2 + k
                    for g in range(GROUPS):
                        if qk:
                            part_after(i, k, g, last)
                        if g == 0:
                            recip(u, k)
                        low(u, g)
                        if not qk:
                            part_after(i, k, g, last)
                        if g == 1 and not (first and k == 0):
                            add_low(u - 1, 1 - k)
            peeled(dve, BODY, body)
            add_low(T - 1, 1)

        @block.scalar
        def _(act):
            def exp(u, k, part=0):
                act.wait_ge(s["y_ready"], u + 1)
                wait(act, s["t_done"], GROUPS * (u - 1))
                wait(act, s["recip"], u - 1)
                cols = slice(part * N // EXPS, (part + 1) * N // EXPS)
                c = EXPS * k + part
                nc.scalar.activation(X[:, k, cols], b.Y[:, k, cols], ACT.Exp, bias=b.ymin[:, k:k + 1], scale=-1.0,
                                     accum_out=b.den[:, c:c + 1]).then_inc(s["e_ready"], 1)

            def normalise(u, k, i):
                act.wait_ge(s["pv_done"], GROUPS * (u + 1))
                act.wait_ge(s["recip"], u + 1)
                wait(act, s[f"out_kept{k}"], 16 * i)
                nc.scalar.activation(b.out[:, k, :], b.bank[4 + k][:, 0:D], ACT.Copy,
                                     scale=b.rden[:, k:k + 1]).then_inc(s["half_out"], 1)

            for part in range(EXPS):
                exp(0, 0, part)

            def body(i, first, last):
                for k in range(2):
                    u = i * 2 + k
                    for g in range(GROUPS):
                        n = u * GROUPS + g
                        act.wait_ge(s["t_done"], n + 1)
                        wait(act, s["pv_done"], n - 1)
                        nc.scalar.activation(b.PH[:, g % 2, :], b.tp[g % 2][:, :], ACT.Copy).then_inc(s["h_ready"], 1)
                        if g == 1 and not (first and k == 0):
                            normalise(u - 1, 1 - k, i if k == 1 else i - 1)
                        if not qk and g in (1, 2) and not (last and k == 1):
                            exp(u + 1, 1 - k, g - 1)
                    if qk and not (last and k == 1):
                        exp(u + 1, 1 - k)
            peeled(act, BODY, body)
            normalise(T - 1, 1, BODY - 1)

        @block.tensor
        def _(pe):
            def transposes(u, k, g):
                n = u * GROUPS + g
                if g % (GROUPS // EXPS) == 0:
                    pe.wait_ge(s["e_ready"], EXPS * u + g * EXPS // GROUPS + 1)
                wait(pe, s["l_ready"], n - 1)
                for q in range(GT):
                    j = g * GT + q
                    mm = nc.tensor.transpose(b.tp[g % 2][:, q * P:(q + 1) * P], X[:, k, j * P:(j + 1) * P], b.ident[:])
                mm.then_inc(s["t_done"], 1)

            def values(u, k, g):
                pe.wait_ge(s["l_ready"], u * GROUPS + g + 1)
                if g == 0:
                    wait(pe, s["out_ready"], u - 1)
                for q in range(GT):
                    j = g * GT + q
                    cols = slice(q * P, (q + 1) * P)

                    def high_part():
                        return nc.tensor.matmul(b.bank[4 + k][:, 0:2 * D], b.PH[:, g % 2, cols],
                                                b.V2[:, j, :, :].rearrange("p a n -> p (a n)"), start=j == 0, stop=j == T - 1)

                    def low_part():
                        return nc.tensor.matmul(b.bank[4 + k][:, 0:D], b.PL[:, g % 2, cols], b.V2[:, j, 0, :],
                                                start=False, stop=False)
                    if j < T - 1:
                        high_part()
                        mm = low_part()
                    else:
                        low_part()
                        mm = high_part()
                mm.then_inc(s["pv_done"], 1)

            def scores(i, k, c):
                u = i * 2 + k
                if c == 0:
                    pe.wait_ge(s[f"q_in{k}"], 16 * (i + 1))
                wait(pe, s["part"], u * GROUPS * SPG + c - 1)
                cols = slice(c * SCH, (c + 1) * SCH)
                for n, (qp, kp) in enumerate(((0, 0), (0, 1), (1, 0))):
                    for d in range(DC):
                        mm = nc.tensor.matmul(b.bank[6 + c % 2][:, :], b.qT2[:, k, qp, d, :], b.KT2[:, kp, d, cols],
                                              start=n == 0 and d == 0, stop=n == 2 and d == DC - 1)
                mm.then_inc(s["s_done"], 1)

            if qk:
                for c in range(GROUPS * SPG):
                    scores(0, 0, c)
            else:
                for g in range(2):
                    transposes(0, 0, g)

            def body(i, first, last):
                for k in range(2):
                    u = i * 2 + k

                    def next_scores(g):
                        if qk and not (last and k == 1):
                            for c in range(SPG * g, SPG * (g + 1)):
                                scores(i + k, 1 - k, c)
                    if not qk:
                        for g in range(GROUPS):
                            if g < 2:
                                transposes(u, k, g + 2)
                            elif not (last and k == 1):
                                transposes(u + 1, 1 - k, g - 2)
                            values(u, k, g)
                        continue
                    transposes(u, k, 0)
                    next_scores(0)
                    transposes(u, k, 1)
                    next_scores(1)
                    values(u, k, 0)
                    transposes(u, k, 2)
                    next_scores(2)
                    values(u, k, 1)
                    transposes(u, k, 3)
                    next_scores(3)
                    values(u, k, 2)
                    values(u, k, 3)
            peeled(pe, BODY, body)


def graph_layers(nc, x, adj, W0, a1, a2, Wr, br, gamma, beta, W1, a, a_row, Wq, Wk, Wv, out):
    with ExitStack() as ctx:
        def dram(name, shape, dt=F32):
            return nc.dram_tensor(name, shape, dt, kind="Internal").ap()

        def sb(scope, name, shape, dt=F32):
            return scope.enter_context(nc.sbuf_tensor(name, shape, dt))

        b = Buffers()
        b.passed_dve = ctx.enter_context(nc.semaphore("passed_dve"))
        b.passed_pool = ctx.enter_context(nc.semaphore("passed_pool"))
        b.adj = adj
        b.pen_dram = dram("pen_dram", (N, N), BF16)
        b.o_dram = dram("o_dram", (N, D))
        b.res_dram = dram("res_dram", (N, D))
        b.rows_dram = dram("rows_dram", (2 * HEADS, N))
        b.q_dram = dram("q_dram", (BODY, P, 2, DC, 2 * P), F32)
        x1, x2, x3 = (dram(f"x{n}_dram", (N, D)) for n in (1, 2, 3))

        psum = ctx.enter_context(nc.psum_tensor("psum", [P, 8, 512], F32))
        b.bank = [psum[:, k, :] for k in range(8)]
        b.tp = [psum[:, 2 * k:2 * k + 2, :].rearrange("p a n -> p (a n)") for k in range(2)]

        b.ident = sb(ctx, "ident", [P, P])
        b.halves = sb(ctx, "halves", [P, F])
        b.diag_big = sb(ctx, "diag_big", [P, P], BF16)
        b.big_col = sb(ctx, "big_col", [P, 1])
        b.minus_half = sb(ctx, "minus_half", [P, 1])
        b.col = sb(ctx, "col", [P, T, HEADS])
        b.Y = sb(ctx, "Y", [P, 2, N])
        b.pen = sb(ctx, "pen", [P, 2, N], BF16)
        b.out = sb(ctx, "out_tile", [P, 2, D])
        b.ymin = sb(ctx, "ymin", [P, 4])
        b.ymin8 = sb(ctx, "ymin8", [P, 2, N // SCH])
        b.den, b.rden, b.lone, b.sums = (sb(ctx, n, [P, 4]) for n in ("den", "rden", "lone", "sums"))

        def parts(buffer, *shapes):
            whole = buffer[:].rearrange("p a n -> p (a n)")
            at, cut = 0, []
            for shape in shapes:
                size = 1
                for n in shape:
                    size *= n
                ap = whole[:, at:at + size]
                at += size
                if len(shape) > 1:
                    letters = "abcd"[:len(shape)]
                    ap = ap.rearrange(f"p ({' '.join(letters)}) -> p {' '.join(letters)}", **dict(zip(letters, shape)))
                cut.append(ap)
            return cut

        (b.xs, b.x_old, b.o_tile, b.xT, b.row_tile, b.stats, b.mv, b.wx, b.wrow, b.wsum, b.wq, b.wk) = parts(
            b.Y, (2, 2, D), (2, 2, D), (2, 2, D), (2, DC, 2 * P), (2, 2 * P), (2, 2, 6), (2, 2, 4), (DC, D + HEADS),
            (DC, 2 * HEADS), (DC, 2, HEADS), (DC, D), (DC, D))
        taken = []

        def sem(name):
            taken.append(nc.alloc_semaphore(name=name))
            return taken[-1]

        def stage(make, *args):
            make(nc, b, sem, *args)
            nc.clear_and_free_semaphores(taken)
            nc.all_engine_barrier()
            taken.clear()

        stage(constants)
        with ExitStack() as gat:
            b.brow = sb(gat, "brow", [P, 4, N])
            b.V = sb(gat, "V", [P, T, D])
            b.E = sb(gat, "E", [P, 2, N])
            b.adj_chunk = sb(gat, "adj_chunk", [P, 2, GW], I32)
            b.PT = sb(gat, "PT", [P, GROUPS, GW])
            b.oT = sb(gat, "oT", [P, 2, P])
            b.res_tile, b.elu, b.wres, b.gamma2, b.beta2, b.br, b.avec, b.wprod = parts(
                b.E, (2, 2, D), (2, 2, D), (DC, D), (2, D), (2, D), (D,), (2, D), (D,))
            stage(gat_weights, "g0", W0, a2, a1)
            stage(dense_weights, "d0", [(b.wres, Wr), (b.br, br)])
            stage(tiles_of_rows, "r0", x, None, None, "gat")
            stage(gat_attention, "a00", 0, 0, True)
            stage(gat_attention, "a01", 0, 1, False)
            stage(gat_weights, "g1", W1, a[:, 0:F], a[:, F:2 * F])
            stage(dense_weights, "d1", [(b.gamma2[:, 0, :], gamma), (b.gamma2[:, 1, :], gamma),
                                        (b.beta2[:, 0, :], beta), (b.beta2[:, 1, :], beta)])
            stage(tiles_of_rows, "r1", x, x1, 0, "gat")
            stage(gat_attention, "a10", 1, 0, False)
            stage(gat_attention, "a11", 1, 1, False)
        with ExitStack() as row:
            b.brow = sb(row, "brow2", [P, 2, N])
            b.V2 = sb(row, "V2", [P, T, 2, D], F32R)
            b.E = sb(row, "E2", [P, 2, N])
            b.PH, b.PL = (sb(row, n, [P, 2, GW], F32R) for n in ("PH2", "PL2"))
            stage(row_weights, "g2", a_row)
            stage(tiles_of_rows, "r2", x1, x2, 1, "row")
            stage(row_attention, "a2", 2)
        with ExitStack() as qkv:
            b.KT2 = sb(qkv, "KT3", [P, 2, DC, N], F32R)
            b.V2 = sb(qkv, "V3", [P, T, 2, D], F32R)
            b.PH, b.PL = (sb(qkv, n, [P, 2, GW], F32R) for n in ("PH3", "PL3"))
            b.qT2 = sb(qkv, "qT3", [P, 2, 2, DC, P], F32R)
            b.q_stage = b.PH[:].rearrange("p a (h c n) -> p a h c n", h=2, c=DC)
            stage(dense_weights, "g3", [(b.wx[:, :, 0:D], Wv), (b.wq, Wq), (b.wk, Wk)])
            stage(tiles_of_rows, "r3", x2, x3, 2, "qkv")
            stage(row_attention, "a3", 3)
            stage(tiles_of_rows, "r4", x3, out, 3, None)


_INS = ["x", "adj", "L0_gnn_W", "L0_gnn_a1", "L0_gnn_a2", "L0_gnn_Wr", "L0_gnn_br", "L0_gnn_gamma", "L0_gnn_beta",
        "L1_gnn_W", "L1_gnn_a", "L2_gnn_a", "L3_gnn_Wq", "L3_gnn_Wk", "L3_gnn_Wv"]
_OUTS = [((N, D), "float32")]


def kernel(**inputs):
    import numpy as _np
    import concourse.bacc as _bacc
    from concourse import mybir as _mybir
    from concourse.bass_utils import run_bass_kernel_spmd as _run

    nc = _bacc.Bacc("TRN2", target_bir_lowering=False, num_devices=1)
    arrays, args = {}, []
    for name in _INS:
        v = _np.ascontiguousarray(inputs[name])
        arrays[f"in_{name}_dram"] = v
        args.append(nc.dram_tensor(f"in_{name}_dram", v.shape, _mybir.dt.from_np(v.dtype), kind="ExternalInput").ap())
    for i, (shape, dtype) in enumerate(_OUTS):
        dt = _mybir.dt.from_np(_np.dtype(dtype))
        args.append(nc.dram_tensor(f"out_{i}_dram", shape, dt, kind="ExternalOutput").ap())
    graph_layers(nc, *args)
    r = _run(nc, [arrays], core_ids=[0])
    return r.results[0]["out_0_dram"]
```

```python
from contextlib import ExitStack

import concourse.bass as bass
from concourse import mybir

F32 = mybir.dt.float32
BF16 = mybir.dt.bfloat16
I32 = mybir.dt.int32
F32R = mybir.dt.float32r
ALU = mybir.AluOpType
ACT = mybir.ActivationFunctionType
AX_X = mybir.AxisListType.X

P = 128
N = 4096
D = 256
HEADS = 4
F = D // HEADS
T = N // P
DC = D // P
PAIRS = HEADS // 2
BODY = T // 2
GROUPS = 4
GW = N // GROUPS
GT = GW // P
SCH = 512
BIG = 2.0 ** 100
LN_EPS = 1e-5
GAT_SLOPE = 0.2
ROW_SLOPE = 0.01


def wait(eng, sem, count):
    if isinstance(count, int) and count <= 0:
        return
    eng.wait_ge(sem, count)


def peeled(eng, n, body):
    body(0, first=True, last=False)
    with eng.Fori(1, n - 1) as i:
        body(i, first=False, last=False)
    body(n - 1, first=False, last=True)


class Semaphores:

    def __init__(self, sem, name):
        self.sem, self.name, self.made = sem, name, {}

    def __getitem__(self, what):
        if what not in self.made:
            self.made[what] = self.sem(f"{self.name}_{what}")
        return self.made[what]


class Buffers:
    pass


def constants(nc, b, sem):
    made = sem("const_made")
    with nc.Block() as block:
        @block.gpsimd
        def _(pool):
            nc.gpsimd.memset(b.ident[:], 0.0).then_inc(made, 1)
            nc.gpsimd.memset(b.halves[:], 0.0).then_inc(made, 1)
            nc.gpsimd.memset(b.diag_big[:], 0.0).then_inc(made, 1)
            nc.gpsimd.memset(b.big_col[:], BIG).then_inc(made, 1)
            nc.gpsimd.memset(b.minus_half[:], -0.5).then_inc(made, 1)
            pool.wait_ge(made, 5)
            nc.gpsimd.affine_select(out=b.ident[:], in_=b.ident[:], compare_op=ALU.not_equal, fill=1.0, base=0,
                                    pattern=[[-1, P]], channel_multiplier=1).then_inc(made, 1)
            nc.gpsimd.affine_select(out=b.diag_big[:], in_=b.diag_big[:], compare_op=ALU.not_equal, fill=BIG, base=0,
                                    pattern=[[-1, P]], channel_multiplier=1).then_inc(made, 1)
            nc.gpsimd.affine_select(out=b.halves[:], in_=b.halves[:], compare_op=ALU.not_equal, fill=1.0, base=0,
                                    pattern=[[-1, F]], channel_multiplier=1).then_inc(made, 1)
            pool.wait_ge(made, 8)
            nc.gpsimd.affine_select(out=b.halves[:], in_=b.halves[:], compare_op=ALU.not_equal, fill=1.0, base=-F,
                                    pattern=[[-1, F]], channel_multiplier=1).then_inc(made, 1)
            pool.wait_ge(made, 9)


def gat_weights(nc, b, sem, name, W, a_self, a_other):
    loaded, did = sem(f"{name}_w_loaded"), sem(f"{name}_w_did")
    with nc.Block() as block:
        @block.sync
        def _(sp):
            for c in range(DC):
                sp.dma_start(b.wx[:, c, 0:D].rearrange("p (h k) -> p h k", h=HEADS),
                             W[:, c * P:(c + 1) * P, :].rearrange("h p k -> p h k")).then_inc(loaded, 16)
            sp.dma_start(b.avec[:, 0, :].rearrange("p (h k) -> p h k", h=HEADS),
                         a_self.partition_broadcast(P)).then_inc(loaded, 16)
            sp.dma_start(b.avec[:, 1, :].rearrange("p (h k) -> p h k", h=HEADS),
                         a_other.partition_broadcast(P)).then_inc(loaded, 16)

        @block.vector
        def _(dve):
            dve.wait_ge(loaded, 16 * (DC + 2))
            n = 0
            for c in range(DC):
                for s in range(2):
                    if n:
                        dve.wait_ge(did, n)
                    nc.vector.tensor_tensor(b.wprod[:], b.wx[:, c, 0:D], b.avec[:, s, :], ALU.mult).then_inc(did, 1)
                    dve.wait_ge(did, n + 1)
                    nc.vector.tensor_reduce(b.wsum[:, c, s, :], b.wprod[:].rearrange("p (h k) -> p h k", h=HEADS),
                                            AX_X, ALU.add).then_inc(did, 1)
                    n += 2
            dve.wait_ge(did, n)
            for c in range(DC):
                nc.vector.tensor_scalar(b.wx[:, c, D:D + HEADS], b.wsum[:, c, 0, :], -(1 - GAT_SLOPE), None,
                                        ALU.mult).then_inc(did, 1)
                nc.vector.tensor_scalar(b.wrow[:, c, 0:HEADS], b.wsum[:, c, 1, :], -1.0, None,
                                        ALU.mult).then_inc(did, 1)
                nc.vector.tensor_scalar(b.wrow[:, c, HEADS:2 * HEADS], b.wsum[:, c, 1, :], -GAT_SLOPE, None,
                                        ALU.mult).then_inc(did, 1)
            dve.wait_ge(did, n + 3 * DC)


def row_weights(nc, b, sem, name, a):
    loaded, did = sem(f"{name}_w_loaded"), sem(f"{name}_w_did")
    with nc.Block() as block:
        @block.sync
        def _(sp):
            sp.dma_start(b.wsum[:].rearrange("p c s h -> p (c s h)")[:, 0:2 * DC],
                         a.rearrange("(s p) one -> p (s one)", p=P), allow_slow_non_contiguous=True).then_inc(loaded, 16)

        @block.vector
        def _(dve):
            dve.wait_ge(loaded, 16)
            cols = b.wsum[:].rearrange("p c s h -> p (c s h)")
            for c in range(DC):
                nc.vector.tensor_scalar(b.wx[:, c, D:D + 1], cols[:, c:c + 1], -(1 - ROW_SLOPE), None,
                                        ALU.mult).then_inc(did, 1)
                nc.vector.tensor_scalar(b.wrow[:, c, 0:1], cols[:, DC + c:DC + c + 1], -1.0, None,
                                        ALU.mult).then_inc(did, 1)
                nc.vector.tensor_scalar(b.wrow[:, c, 1:2], cols[:, DC + c:DC + c + 1], -ROW_SLOPE, None,
                                        ALU.mult).then_inc(did, 1)
            dve.wait_ge(did, 3 * DC)


def dense_weights(nc, b, sem, name, pairs):
    loaded = sem(f"{name}_dense_loaded")
    with nc.Block() as block:
        @block.sync
        def _(sp):
            for dst, src in pairs:
                if len(src.shape) == 1:
                    sp.dma_start(dst, src.partition_broadcast(P)).then_inc(loaded, 16)
                else:
                    sp.dma_start(dst, src.rearrange("(c p) n -> p c n", p=P)).then_inc(loaded, 16)
            sp.wait_ge(loaded, 16 * len(pairs))


def tiles_of_rows(nc, b, sem, name, x_in, kind, res=False):
    s = Semaphores(sem, name)
    n_rows = {"gat": 2 * HEADS, "row": 2}.get(kind, 0)
    xin = x_in.rearrange("(g k p) d -> g p k d", p=P, k=2)
    res_out = b.res_dram.rearrange("(g k p) d -> g p k d", p=P, k=2)
    rows_out = b.rows_dram.rearrange("r (g n) -> g r n", n=2 * P)

    def groups(eng, lags, step):
        most = max(lag for _, lag in lags)

        def turn(t, slot, i):
            for what, lag in lags:
                g = t - lag
                if isinstance(t, int) and not 0 <= g < BODY:
                    continue
                step(what, g, (slot - lag) % 2, i - (lag - slot + 1) // 2)
        lead = most + 2 + most % 2
        for t in range(lead):
            turn(t, t % 2, t // 2)
        with eng.Fori(lead // 2, BODY // 2) as i:
            turn(i * 2, 0, i)
            turn(i * 2 + 1, 1, i)
        for t in range(BODY, BODY + most):
            turn(t, t % 2, t // 2)

    def at(g, buf, size=1, *rest):
        if isinstance(g, int):
            return buf[(slice(None), slice(size * g, size * (g + 1))) + rest]
        return buf[(slice(None), bass.ds(g * size, size)) + rest]

    def transposed(n):
        return s["xT_bank"], DC * n

    def projected(n):
        if res:
            return s["res"], 2 * n
        return s["rows"], (DC if kind == "qkv" else 1) * n

    with nc.Block() as block:
        @block.sync
        def _(sp):
            def step(what, g, slot, i):
                gg = g if isinstance(g, int) else sp.snap(g)
                if what == "rows_back":
                    sp.wait_ge(s[f"rows_kept{slot}"], 16 * (i + 1))
                    cols = slice(2 * P * g, 2 * P * (g + 1)) if isinstance(g, int) else bass.ds(g * 2 * P, 2 * P)
                    for r in range(b.brow.shape[1]):
                        row = HEADS * (r // 2) + r % 2 if kind == "gat" else r
                        sp.dma_start(b.brow[:, r, cols], rows_out[gg, row, :].partition_broadcast(P)).then_inc(s[f"rows_back{slot}"], 16)
                    return
                wait(sp, *transposed(g - 1))
                if kind == "row":
                    wait(sp, s["v_low"], g - 1)
                sp.dma_start(b.xs[:, slot, :, :], xin[gg, :, :, :]).then_inc(s[f"in{slot}"], 16)
            groups(sp, [("load", 0)] + [("rows_back", 4)] * (kind != "qkv"), step)
            if kind != "qkv":
                for slot in range(2):
                    sp.wait_ge(s[f"rows_back{slot}"], 16 * b.brow.shape[1] * BODY // 2)

        @block.vector
        def _(dve):
            def step(what, g, slot, i):
                if what == "take":
                    for k in range(2):
                        tile = 2 * g + k
                        dve.wait_ge(s["proj"], tile + 1)
                        if kind == "row":
                            nc.vector.tensor_copy(at(tile, b.col, 1, slice(0, 1)),
                                                  b.bank[2 + k][:, D:D + 1].rearrange("p (o n) -> p o n", o=1)).then_inc(s["proj_out"], 1)
                            continue
                        v_psum = b.bank[2 + k][:, 0:D].rearrange("p (o n) -> p o n", o=1)
                        if kind == "gat":
                            nc.vector.tensor_copy(at(tile, b.col, 1, slice(None)),
                                                  b.bank[2 + k][:, D:D + HEADS].rearrange("p (o n) -> p o n", o=1))
                            nc.vector.tensor_copy(at(tile, b.V, 1, slice(None)), v_psum).then_inc(s["proj_out"], 1)
                        if kind == "qkv":
                            dve.wait_ge(s["v_high"], tile + 1)
                            nc.vector.tensor_tensor(at(tile, b.V2, 1, 1, slice(None)), v_psum,
                                                    at(tile, b.V2, 1, 0, slice(None)).bitcast(F32),
                                                    ALU.subtract).then_inc(s["proj_out"], 1)
                    if kind == "qkv":
                        for c in range(DC):
                            dve.wait_ge(s["k_high"], DC * g + c + 1)
                            cols = slice(2 * P * g, 2 * P * (g + 1)) if isinstance(g, int) else bass.ds(g * 2 * P, 2 * P)
                            nc.vector.tensor_tensor(b.KT2[:, 1, c, cols], b.bank[6 + c][:, 0:2 * P],
                                                    b.KT2[:, 0, c, cols].bitcast(F32),
                                                    ALU.subtract).then_inc(s["k_low"], 1)
                            dve.wait_ge(s["q_high"], DC * g + c + 1)
                            if c == 0:
                                wait(dve, s[f"rows_kept{slot}"], 16 * i)
                            nc.vector.scalar_tensor_tensor(b.q_stage[:, slot, 1, c, :], b.bank[4 + c][:, 0:2 * P], -1.0,
                                                           b.q_stage[:, slot, 0, c, :].bitcast(F32), ALU.mult,
                                                           ALU.subtract).then_inc(s["q_low"], 1)
                    if res:
                        wait(dve, s[f"res_kept{slot}"], 16 * i)
                        for k in range(2):
                            dve.wait_ge(s["res"], 2 * g + k + 1)
                            nc.vector.tensor_tensor(b.res_tile[:, slot, k, :], b.bank[6 + k][:, 0:D], b.br[:],
                                                    ALU.add).then_inc(s["res_out"], 1)
            groups(dve, [("take", 2)], step)

        if kind == "row":
            @block.gpsimd
            def _(pool):
                def step(what, g, slot, i):
                    pool.wait_ge(s["v_high"], g + 1)
                    nc.gpsimd.tensor_tensor(at(g, b.V2, 2, 1, slice(None)), b.xs[:, slot, :, :],
                                            at(g, b.V2, 2, 0, slice(None)).bitcast(F32),
                                            ALU.subtract).then_inc(s["v_low"], 1)
                groups(pool, [("v_low", 1)], step)

        @block.scalar
        def _(act):
            def step(what, g, slot, i):
                gg = g if isinstance(g, int) else act.snap(g)
                if what == "xT":
                    for c in range(DC):
                        act.wait_ge(s["xT_bank"], DC * g + c + 1)
                        if c == 0:
                            wait(act, *projected(g - 1))
                        ins = nc.scalar.activation(b.xT[:, slot, c, :], b.bank[c][:, 0:2 * P], ACT.Copy)
                        ins.then_inc(s["xT_sbuf"], 1)
                    if kind == "row":
                        nc.scalar.activation(at(g, b.V2, 2, 0, slice(None)), b.xs[:, slot, :, :],
                                             ACT.Copy).then_inc(s["v_high"], 1)
                if what == "take":
                    if kind == "qkv":
                        for k in range(2):
                            act.wait_ge(s["proj"], 2 * g + k + 1)
                            nc.scalar.activation(at(2 * g + k, b.V2, 1, 0, slice(None)),
                                                 b.bank[2 + k][:, 0:D].rearrange("p (o n) -> p o n", o=1),
                                                 ACT.Copy).then_inc(s["v_high"], 1)
                        for c in range(DC):
                            cols = slice(2 * P * g, 2 * P * (g + 1)) if isinstance(g, int) else bass.ds(g * 2 * P, 2 * P)
                            act.wait_ge(s["keys"], DC * g + c + 1)
                            nc.scalar.activation(b.KT2[:, 0, c, cols], b.bank[6 + c][:, 0:2 * P],
                                                 ACT.Copy).then_inc(s["k_high"], 1)
                            act.wait_ge(s["rows"], DC * g + c + 1)
                            if c == 0:
                                wait(act, s[f"rows_kept{slot}"], 16 * i)
                            nc.scalar.activation(b.q_stage[:, slot, 0, c, :], b.bank[4 + c][:, 0:2 * P], ACT.Copy,
                                                 scale=-1.0).then_inc(s["q_high"], 1)
                        act.wait_ge(s["q_low"], DC * (g + 1))
                        act.dma_start(b.q_dram[gg, :, :, :, :], b.q_stage[:, slot, :, :, :].bitcast(F32)).then_inc(s[f"rows_kept{slot}"], 16)
                    else:
                        act.wait_ge(s["rows"], g + 1)
                        wait(act, s[f"rows_kept{slot}"], 16 * i)
                        nc.scalar.activation(b.row_tile[0:n_rows, slot, :], b.bank[4 + slot][0:n_rows, 0:2 * P],
                                             ACT.Copy).then_inc(s["rows_out"], 1)
                        act.wait_ge(s["rows_out"], g + 1)
                        act.dma_start(rows_out[gg, 0:n_rows, :], b.row_tile[0:n_rows, slot, :]).then_inc(s[f"rows_kept{slot}"], 16)
                if what == "keep_res":
                    act.wait_ge(s["res_out"], 2 * (g + 1))
                    act.dma_start(res_out[gg, :, :, :], b.res_tile[:, slot, :, :]).then_inc(s[f"res_kept{slot}"], 16)
            lags = [("xT", 1), ("take", 2)]
            if res:
                lags += [("keep_res", 2)]
            groups(act, lags, step)
            for slot in range(2):
                act.wait_ge(s[f"rows_kept{slot}"], 16 * BODY // 2)
                if res:
                    act.wait_ge(s[f"res_kept{slot}"], 16 * BODY // 2)

        @block.tensor
        def _(pe):
            def step(what, g, slot, i):
                if what == "xT":
                    pe.wait_ge(s[f"in{slot}"], 16 * (i + 1))
                    for c in range(DC):
                        wait(pe, s["xT_sbuf"], DC * (g - 1) + c + 1)
                        for k in range(2):
                            mm = nc.tensor.transpose(b.bank[c][:, k * P:(k + 1) * P],
                                                     b.xs[:, slot, k, c * P:(c + 1) * P], b.ident[:])
                        mm.then_inc(s["xT_bank"], 1)
                if what == "project":
                    pe.wait_ge(s["xT_sbuf"], DC * (g + 1))
                    a, z = {"gat": (0, D + HEADS), "row": (D, D + 1), "qkv": (0, D)}[kind]
                    for k in range(2):
                        wait(pe, s["proj_out"], 2 * (g - 1) + k + 1)
                        for c in range(DC):
                            mm = nc.tensor.matmul(b.bank[2 + k][:, a:z], b.xT[:, slot, c, k * P:(k + 1) * P],
                                                  b.wx[:, c, a:z], start=c == 0, stop=c == DC - 1)
                        mm.then_inc(s["proj"], 1)
                    if kind == "qkv":
                        for w, bank, made, taken in ((b.wk, 6, "keys", "k_low"), (b.wq, 4, "rows", "q_low")):
                            for half in range(DC):
                                wait(pe, s[taken], DC * (g - 1) + half + 1)
                                for c in range(DC):
                                    mm = nc.tensor.matmul(b.bank[bank + half][:, 0:2 * P],
                                                          w[:, c, half * P:(half + 1) * P], b.xT[:, slot, c, :],
                                                          start=c == 0, stop=c == DC - 1)
                                mm.then_inc(s[made], 1)
                    else:
                        wait(pe, s["rows_out"], g - 1)
                        for c in range(DC):
                            mm = nc.tensor.matmul(b.bank[4 + slot][0:n_rows, 0:2 * P], b.wrow[:, c, 0:n_rows],
                                                  b.xT[:, slot, c, :], start=c == 0, stop=c == DC - 1)
                        mm.then_inc(s["rows"], 1)
                    if res:
                        for k in range(2):
                            wait(pe, s["res_out"], 2 * (g - 1) + k + 1)
                            for c in range(DC):
                                mm = nc.tensor.matmul(b.bank[6 + k][:, 0:D], b.xT[:, slot, c, k * P:(k + 1) * P],
                                                      b.wres[:, c, :], start=c == 0, stop=c == DC - 1)
                            mm.then_inc(s["res"], 1)
            groups(pe, [("xT", 0), ("project", 1)], step)


def column(b, tile, h):
    if isinstance(tile, int):
        return b.col[:, tile:tile + 1, h:h + 1].rearrange("p o h -> p (o h)")
    return b.col[:, bass.ds(tile, 1), h:h + 1].rearrange("p o h -> p (o h)")


class Finish:

    def __init__(self, nc, b, s, x_in, x_out, half):
        self.nc, self.b, self.s, self.half = nc, b, s, half
        self.x_in, self.x_out, self.o_in = (a.rearrange("(t p) d -> t p d", p=P) for a in (x_in, x_out, b.o_dram))

    def load(self, pool, u, k):
        t = u if isinstance(u, int) else pool.snap(u)
        pool.dma_start(self.b.x_tile[:, k, :], self.x_in[t, :, :]).then_inc(self.s[f"x_in{k}"], 16)
        if self.half:
            pool.dma_start(self.b.o_half[:, k, :], self.o_in[t, :, 0:D // 2]).then_inc(self.s[f"x_in{k}"], 16)

    def add_x(self, pool, k, i, ready, count):
        b, nc = self.b, self.nc
        pool.wait_ge(ready, count)
        pool.wait_ge(self.s[f"x_in{k}"], 16 * (2 if self.half else 1) * (i + 1))
        if self.half:
            nc.gpsimd.tensor_tensor(b.out[:, k, 0:D // 2], b.o_half[:, k, :], b.x_tile[:, k, 0:D // 2],
                                    ALU.add).then_inc(self.s["with_x"], 1)
            nc.gpsimd.tensor_tensor(b.out[:, k, D // 2:D], b.out[:, k, D // 2:D], b.x_tile[:, k, D // 2:D],
                                    ALU.add).then_inc(self.s["with_x"], 1)
        else:
            nc.gpsimd.tensor_tensor(b.out[:, k, :], b.out[:, k, :], b.x_tile[:, k, :], ALU.add).then_inc(
                self.s["with_x"], 1)

    def moments(self, dve, u, k, ready, count):
        b, nc = self.b, self.nc
        dve.wait_ge(ready, count)
        nc.vector.bn_stats(b.row_stats[:, k, :], b.out[:, k, :]).then_inc(self.s["stats"], 1)
        dve.wait_ge(self.s["stats"], u + 1)
        dve.sem_inc(b.passed_dve, 1)
        nc.vector.bn_aggr(b.moments[:, k, 0:2], b.row_stats[:, k, :]).then_inc(self.s["moments"], 1)

    def scale_shift(self, pool, u, k):
        b, nc = self.b, self.nc
        pool.wait_ge(self.s["moments"], u + 1)
        pool.sem_inc(b.passed_pool, 1)
        nc.gpsimd.tensor_scalar(b.moments[:, k, 2:3], b.moments[:, k, 1:2], LN_EPS, None,
                                ALU.add).then_inc(self.s["eps"], 1)
        nc.gpsimd.tensor_scalar(b.moments[:, k, 4:5], b.moments[:, k, 0:1], -1.0, None,
                                ALU.mult).then_inc(self.s["eps"], 1)
        pool.wait_ge(self.s["eps"], 2 * (u + 1))
        nc.gpsimd.tensor_tensor(b.moments[:, k, 3:4], b.moments[:, k, 2:3], b.minus_half[:],
                                ALU.pow).then_inc(self.s["rstd"], 1)
        pool.wait_ge(self.s["rstd"], u + 1)
        nc.gpsimd.tensor_tensor(b.moments[:, k, 5:6], b.moments[:, k, 4:5], b.moments[:, k, 3:4],
                                ALU.mult).then_inc(self.s["shift"], 1)

    def finish(self, act, u, k):
        b, nc = self.b, self.nc
        act.wait_ge(self.s["shift"], u + 1)
        nc.scalar.activation(b.out[:, k, :], b.out[:, k, :], ACT.Identity, bias=b.moments[:, k, 5:6],
                             scale=b.moments[:, k, 3:4]).then_inc(self.s["finished"], 1)

    def keep(self, pool, u, k):
        t = u if isinstance(u, int) else pool.snap(u)
        pool.wait_ge(self.s["finished"], u + 1)
        pool.dma_start(self.x_out[t, :, :], self.b.out[:, k, :]).then_inc(self.s[f"out_kept{k}"], 16)


class EluFinish:
    LAG = 3

    def __init__(self, nc, b, s, x_in, x_out, gamma, beta):
        self.nc, self.b, self.s, self.gamma, self.beta = nc, b, s, gamma, beta
        self.x_in, self.x_out, self.o_in, self.res_in = (
            a.rearrange("(t p) d -> t p d", p=P) for a in (x_in, x_out, b.o_dram, b.res_dram))

    def there(self, u):
        return not isinstance(u, int) or 0 <= u < T

    def load_attention(self, pool, u):
        t = u if isinstance(u, int) else pool.snap(u)
        pool.dma_start(self.b.o_half, self.o_in[t, :, 0:D // 2]).then_inc(self.s["o_in"], 16)
        pool.dma_start(self.b.res, self.res_in[t, :, :]).then_inc(self.s["o_in"], 16)

    def load_x(self, pool, u):
        t = u if isinstance(u, int) else pool.snap(u)
        pool.dma_start(self.b.x_one, self.x_in[t, :, :]).then_inc(self.s["x_in"], 16)

    def start(self, pool):
        pool.wait_ge(self.s["pen_made"], GROUPS * T)
        pool.dma_start(self.b.gamma, self.gamma.partition_broadcast(P)).then_inc(self.s["affine_in"], 16)
        pool.dma_start(self.b.beta, self.beta.partition_broadcast(P)).then_inc(self.s["affine_in"], 16)
        self.load_attention(pool, 0)
        self.load_x(pool, 0)
        pool.wait_ge(self.s["affine_in"], 32)

    def act_elu(self, act, u, k):
        b, nc, s = self.b, self.nc, self.s
        act.wait_ge(s["o_in"], 32 * (u + 1))
        act.wait_ge(s["out_ready"], 2 * (u + T + 1))
        wait(act, s["summed"], u)
        nc.scalar.activation(b.elu[:, 0:D // 2], b.o_half, ACT.Relu, scale=-1.0).then_inc(s["relu"], 1)
        nc.scalar.activation(b.elu[:, D // 2:D], b.out[:, k, D // 2:D], ACT.Relu, scale=-1.0).then_inc(s["relu"], 1)
        act.wait_ge(s["relu"], 2 * (u + 1))
        nc.scalar.activation(b.elu, b.elu, ACT.Exp, scale=-1.0).then_inc(s["elu_exp"], 1)

    def act_scale(self, act, u, k, shift, done):
        b, nc = self.b, self.nc
        act.wait_ge(self.s[shift], u + 1)
        nc.scalar.activation(b.sum[:, k, :], b.sum[:, k, :], ACT.Identity, bias=b.moments[:, k, 5:6],
                             scale=b.moments[:, k, 3:4]).then_inc(self.s[done], 1)

    def act_outer_norm(self, act, t, k):
        if self.there(t - 3):
            self.act_scale(act, t - 3, 1 - k, "shift2", "finished")

    def act_own_norm(self, act, t, k):
        if self.there(t - 2):
            self.act_scale(act, t - 2, k, "shift1", "norm1")

    def act_exp(self, act, t, k):
        if self.there(t - 1):
            self.act_elu(act, t - 1, 1 - k)

    def spread(self, dve, u, k, which):
        self.nc.vector.bn_stats(self.b.row_stats[:, k, :], self.b.sum[:, k, :]).then_inc(self.s["stats" + which], 1)

    def moments(self, dve, u, k, which):
        dve.wait_ge(self.s["stats" + which], u + 1)
        dve.sem_inc(self.b.passed_dve, 1)
        self.nc.vector.bn_aggr(self.b.moments[:, k, 0:2], self.b.row_stats[:, k, :]).then_inc(
            self.s["moments" + which], 1)

    def dve_turn(self, dve, t, k, i):
        b, nc, s = self.b, self.nc, self.s
        if self.there(t - 2):
            u = t - 2
            dve.wait_ge(s["elu_exp"], u + 1)
            nc.vector.scalar_tensor_tensor(b.elu[:, 0:D // 2], b.o_half, 0.0, b.elu[:, 0:D // 2], ALU.max,
                                           ALU.add).then_inc(s["elu_max"], 1)
            nc.vector.scalar_tensor_tensor(b.elu[:, D // 2:D], b.out[:, k, D // 2:D], 0.0, b.elu[:, D // 2:D], ALU.max,
                                           ALU.add).then_inc(s["elu_max"], 1)
        if self.there(t - 3):
            dve.wait_ge(s["affine"], t - 2)
            self.spread(dve, t - 3, 1 - k, "2")
        if self.there(t - 2):
            dve.wait_ge(s["elu_max"], 2 * (u + 1))
            wait(dve, s[f"x_kept{k}"], 16 * (i - 1))
            nc.vector.scalar_tensor_tensor(b.sum[:, k, :], b.elu, -1.0, b.res, ALU.add,
                                           ALU.add).then_inc(s["summed"], 1)
        if self.there(t - 3):
            self.moments(dve, t - 3, 1 - k, "2")
        if self.there(t - 2):
            dve.wait_ge(s["summed"], u + 1)
            self.spread(dve, u, k, "1")
            self.moments(dve, u, k, "1")

    def scale_shift(self, pool, u, k, which):
        b, nc, s = self.b, self.nc, self.s
        pool.wait_ge(s["moments" + which], u + 1)
        pool.sem_inc(b.passed_pool, 1)
        nc.gpsimd.tensor_scalar(b.moments[:, k, 2:3], b.moments[:, k, 1:2], LN_EPS, None,
                                ALU.add).then_inc(s["eps" + which], 1)
        nc.gpsimd.tensor_scalar(b.moments[:, k, 4:5], b.moments[:, k, 0:1], -1.0, None,
                                ALU.mult).then_inc(s["eps" + which], 1)
        pool.wait_ge(s["eps" + which], 2 * (u + 1))
        nc.gpsimd.tensor_tensor(b.moments[:, k, 3:4], b.moments[:, k, 2:3], b.minus_half[:],
                                ALU.pow).then_inc(s["rstd" + which], 1)
        pool.wait_ge(s["rstd" + which], u + 1)
        nc.gpsimd.tensor_tensor(b.moments[:, k, 5:6], b.moments[:, k, 4:5], b.moments[:, k, 3:4],
                                ALU.mult).then_inc(s["shift" + which], 1)

    def pool_turn(self, pool, t, k):
        b, nc, s = self.b, self.nc, self.s
        if self.there(t - 3):
            self.scale_shift(pool, t - 3, 1 - k, "2")
        if self.there(t - 2):
            self.scale_shift(pool, t - 2, k, "1")
            if self.there(t - 1):
                pool.wait_ge(s["summed"], t - 1)
                pool.sem_inc(b.passed_pool, 1)
                self.load_attention(pool, t - 1)
            pool.wait_ge(s["x_in"], 16 * (t - 1))
            nc.gpsimd.tensor_tensor(b.x_one, b.x_one, b.beta, ALU.add).then_inc(s["x_beta"], 1)
        if self.there(t - 3):
            u = t - 3
            n = u if isinstance(u, int) else pool.snap(u)
            pool.wait_ge(s["finished"], u + 1)
            pool.dma_start(self.x_out[n, :, :], b.sum[:, 1 - k, :]).then_inc(s[f"x_kept{1 - k}"], 16)
        if self.there(t - 2):
            u = t - 2
            pool.wait_ge(s["norm1"], u + 1)
            nc.gpsimd.tensor_tensor(b.sum[:, k, :], b.sum[:, k, :], b.gamma, ALU.mult).then_inc(s["scaled"], 1)
            pool.wait_ge(s["scaled"], u + 1)
            pool.wait_ge(s["x_beta"], u + 1)
            nc.gpsimd.tensor_tensor(b.sum[:, k, :], b.sum[:, k, :], b.x_one, ALU.add).then_inc(s["affine"], 1)
            if self.there(t - 1):
                pool.wait_ge(s["affine"], u + 1)
                pool.sem_inc(b.passed_pool, 1)
                self.load_x(pool, t - 1)


def both_pairs(eng, body, lead):
    for pair in range(PAIRS):
        start = pair * BODY
        for i in range(lead):
            body(start + i, pair, first=i == 0, last=False)
        with eng.Fori(start + lead, start + BODY - 1) as i:
            body(i, pair, first=False, last=False)
        body(start + BODY - 1, pair, first=False, last=True)


def gat_attention(nc, b, sem, name, layer, x_in, x_out, *gamma_beta):
    s = Semaphores(sem, name)
    pen_t = b.pen_dram.rearrange("(t p) j -> t p j", p=P)
    adj_t = b.adj.rearrange("(t p) j -> t p j", p=P)
    o_t = b.o_dram.rearrange("(t p) d -> t p d", p=P)
    UNITS = 4
    ALL = PAIRS * BODY * UNITS
    fin = Finish(nc, b, s, x_in, x_out, half=True) if layer == 1 else None
    elu = EluFinish(nc, b, s, x_in, x_out, *gamma_beta) if layer == 0 else None
    LEAD = 1 if fin else 2

    def makes_penalties(pair):
        return layer == 0 and pair == 0

    def number(eng, n):
        return n if isinstance(n, int) else eng.snap(n)

    def penalties_in(i, k):
        return s[f"pen_in{k}"], 16 * (i + 1 - (BODY if layer == 0 else 0))

    with nc.Block() as block:
        @block.sync
        def _(sp):
            def load_rows(hh):
                for q in range(2):
                    sp.dma_start(b.brow[:, 2 * q + hh, :],
                                 b.rows_dram[HEADS * q + 2 + hh, :].partition_broadcast(P)).then_inc(s[f"rows_in{hh}"], 16)

            def body(i, pair, first, last):
                for k in range(2):
                    tile = i * 2 + k
                    t = number(sp, tile - pair * T)
                    if makes_penalties(pair):
                        for c in range(GROUPS):
                            wait(sp, s["pen_made"], GROUPS * tile + c - 1)
                            sp.dma_start(b.adj_chunk[:, c % 2, :], adj_t[t, :, c * GW:(c + 1) * GW]).then_inc(s[f"adj_in{c % 2}"], 16)
                    else:
                        if layer == 0 and first and k == 0:
                            for slot in range(2):
                                sp.wait_ge(s[f"pen_kept{slot}"], 16 * BODY)
                        wait(sp, s["y_ready"], (tile - 1) * 2)
                        sp.dma_start(b.pen[:, k, :], pen_t[t, :, :]).then_inc(s[f"pen_in{k}"], 16)
                    if first and pair == 1 and k == 0:
                        for hh in range(2):
                            sp.wait_ge(s["y_raw"], 2 * T - 1 + hh)
                            load_rows(hh)
            both_pairs(sp, body, LEAD)

        @block.gpsimd
        def _(pool):
            def lone(u, v):
                pool.wait_ge(s["e_ready"], u + 1)
                wait(pool, s["recip"], u - UNITS + 1)
                pool.sem_inc(b.passed_pool, 1)
                nc.gpsimd.tensor_scalar(b.lone[:, v:v + 1], b.ymin[:, v:v + 1], BIG, 0.0, ALU.mult,
                                        ALU.mult).then_inc(s["lone"], 1)
                pool.wait_ge(s["lone"], u + 1)
                nc.gpsimd.tensor_tensor(b.sums[:, v:v + 1], b.lone[:, v:v + 1], b.den[:, v:v + 1],
                                        ALU.add).then_inc(s["sums"], 1)

            def keep(tile, k, pair):
                t = number(pool, tile - pair * T)
                pool.wait_ge(s["out_ready"], 2 * (tile + 1))
                pool.dma_start(o_t[t, :, pair * 2 * F:(pair + 1) * 2 * F],
                               b.out[:, k, pair * 2 * F:(pair + 1) * 2 * F]).then_inc(s[f"out_kept{k}"], 16)

            def body(i, pair, first, last):
                for k in range(2):
                    tile = i * 2 + k
                    t = tile - pair * T
                    if makes_penalties(pair):
                        pool.wait_ge(s["pen_made"], GROUPS * (tile + 1))
                        pool.dma_start(pen_t[number(pool, t), :, :], b.pen[:, k, :]).then_inc(s[f"pen_kept{k}"], 16)
                    finishes = pair == 1
                    if layer == 1:
                        lone(i * UNITS + 2 * k, 2 * k)
                    if finishes and fin and not first:
                        fin.scale_shift(pool, t - 2, k)
                    if layer == 1:
                        lone(i * UNITS + 2 * k + 1, 2 * k + 1)
                    if first and k == 0:
                        if pair == 1:
                            keep(tile - 1, 1 - k, 0)
                        if finishes:
                            for slot in range(2):
                                pool.wait_ge(s[f"out_kept{slot}"], 16 * BODY)
                            if elu:
                                elu.start(pool)
                            else:
                                for slot in range(2):
                                    fin.load(pool, slot, slot)
                    elif not finishes:
                        keep(tile - 1, 1 - k, pair)
                    elif fin:
                        fin.add_x(pool, 1 - k, (i if k == 1 else i - 1) - BODY, s["out_ready"], 2 * tile)
                        if not (last and k == 1):
                            pool.wait_ge(s["with_x"], 2 * t)
                            fin.load(pool, t + 1, 1 - k)
                        if not first:
                            fin.keep(pool, t - 2, k)
                    if finishes and elu:
                        elu.pool_turn(pool, t, k)

            both_pairs(pool, body, LEAD)
            if fin:
                fin.scale_shift(pool, T - 2, 0)
                fin.keep(pool, T - 2, 0)
                fin.add_x(pool, 1, BODY - 1, s["out_ready"], 2 * 2 * T)
                fin.scale_shift(pool, T - 1, 1)
                fin.keep(pool, T - 1, 1)
            else:
                for t in range(T, T + elu.LAG):
                    elu.pool_turn(pool, t, t % 2)
            for k in range(2):
                if elu:
                    pool.wait_ge(s[f"x_kept{k}"], 16 * BODY)
                else:
                    pool.wait_ge(s[f"out_kept{k}"], 16 * 2 * BODY)

        @block.vector
        def _(dve):
            def recip(u, v):
                dve.wait_ge(s["sums" if layer == 1 else "e_ready"], u + 1)
                sums = b.sums if layer == 1 else b.den
                nc.vector.reciprocal(b.rden[:, v:v + 1], sums[:, v:v + 1]).then_inc(s["recip"], 1)

            def body(i, pair, first, last):
                for v in range(UNITS):
                    u = i * UNITS + v
                    k, hh = v // 2, v % 2
                    tile = i * 2 + k
                    t = tile - pair * T
                    Y = b.Y[:, v % 2, :]
                    if first and pair == 1 and k == 0:
                        dve.wait_ge(s[f"rows_in{hh}"], 16 * 2)
                    wait(dve, s["e_ready"], u - 1)
                    nc.vector.scalar_tensor_tensor(Y, b.brow[:, hh, :], column(b, t, 2 * pair + hh),
                                                   b.brow[:, 2 + hh, :], ALU.add, ALU.min).then_inc(s["y_raw"], 1)
                    if not (first and pair == 0 and v < 2):
                        recip(u - 2, (v - 2) % UNITS)
                    if elu and pair == 1 and hh == 1:
                        elu.dve_turn(dve, t, k, i - BODY)
                    if fin and pair == 1 and hh == 1 and not first:
                        fin.moments(dve, t - 2, k, s["with_x"], 2 * (t - 1))
                    if hh == 0:
                        if makes_penalties(pair):
                            dve.wait_ge(s["pen_made"], GROUPS * (tile + 1))
                        else:
                            dve.wait_ge(*penalties_in(i, k))
                    if layer == 1:
                        wait(dve, s["lone"], u - UNITS + 1)
                    dve.wait_ge(s["y_raw"], u + 1)
                    dve.sem_inc(b.passed_dve, 1)
                    nc.vector.tensor_tensor_reduce(Y, Y, b.pen[:, k, :], 1.0, 3e38, ALU.add, ALU.min,
                                                   b.ymin[:, v:v + 1]).then_inc(s["y_ready"], 1)
            both_pairs(dve, body, LEAD)
            for v in (UNITS - 2, UNITS - 1):
                recip(ALL - UNITS + v, v)
            if fin:
                for k in range(2):
                    fin.moments(dve, T - 2 + k, k, s["with_x"], 2 * (T - 1 + k))
            else:
                for t in range(T, T + elu.LAG):
                    elu.dve_turn(dve, t, t % 2, t // 2)

        @block.scalar
        def _(act):
            def penalty(tile, k, c, kept):
                act.wait_ge(s[f"adj_in{c % 2}"], 16 * (2 * tile + c // 2 + 1))
                if c == 0:
                    wait(act, s["y_ready"], (tile - 1) * 2)
                    wait(act, s[f"pen_kept{k}"], 16 * kept)
                nc.scalar.activation(b.pen[:, k, c * GW:(c + 1) * GW], b.adj_chunk[:, c % 2, :], ACT.Relu,
                                     bias=b.big_col[:, 0:1], scale=-BIG).then_inc(s["pen_made"], 1)

            def exp(u, v):
                act.wait_ge(s["y_ready"], u + 1)
                wait(act, s["t_done"], GROUPS * (u - 1))
                wait(act, s["recip"], u - UNITS + 1)
                nc.scalar.activation(b.E[:, v % 2, :], b.Y[:, v % 2, :], ACT.Exp, bias=b.ymin[:, v:v + 1], scale=-1.0,
                                     accum_out=b.den[:, v:v + 1]).then_inc(s["e_ready"], 1)

            def take_acc(u, slot):
                act.wait_ge(s["pv_done"], GROUPS * (u + 1))
                wait(act, s["o_done"], u - 1)
                nc.scalar.activation(b.oT[:, slot, :], b.bank[4 + slot][:, 0:P], ACT.Copy).then_inc(s["oT_ready"], 1)

            def normalise(u, v, i, pair):
                k, hh = v // 2, v % 2
                act.wait_ge(s["o_done"], u + 1)
                act.wait_ge(s["recip"], u + 1)
                if hh == 0 and (fin or pair == 0):
                    wait(act, s[f"out_kept{k}"], 16 * i)
                elif hh == 0:
                    wait(act, s["summed"], 2 * i + k - T - 1)
                h = 2 * pair + hh
                nc.scalar.activation(b.out[:, k, h * F:(h + 1) * F], b.bank[6 + v % 2][:, 0:F], ACT.Copy,
                                     scale=b.rden[:, v:v + 1]).then_inc(s["out_ready"], 1)

            if layer == 0:
                for c in range(GROUPS):
                    penalty(0, 0, c, 0)
                for c in range(GROUPS // 2):
                    penalty(1, 1, c, 0)
            exp(0, 0)

            def body(i, pair, first, last):
                for v in range(UNITS):
                    u = i * UNITS + v
                    k, hh = v // 2, v % 2
                    before = not (first and pair == 0 and v == 0)
                    if makes_penalties(pair) and hh == 0 and not (last and k == 1):
                        for c in range(GROUPS // 2, GROUPS):
                            penalty(i * 2 + k + 1, 1 - k, c, i + k)
                    if not (last and pair == 1 and v == UNITS - 1):
                        exp(u + 1, (v + 1) % UNITS)
                    if makes_penalties(pair) and hh == 1 and not last:
                        for c in range(GROUPS // 2):
                            penalty(i * 2 + k + 2, k, c, i + 1)
                    if before:
                        take_acc(u - 1, (v - 1) % 2)
                    behind = elu and pair == 1 and hh == 0
                    t = i * 2 + k - pair * T
                    for g in range(GROUPS):
                        n = u * GROUPS + g
                        act.wait_ge(s["t_done"], n + 1)
                        wait(act, s["pv_done"], n - GROUPS + 1)
                        nc.scalar.activation(b.PT[:, g, :], b.tp[g % 2][:, :], ACT.Copy).then_inc(s["pt_ready"], 1)
                        if g == 1 and before:
                            normalise(u - 1, (v - 1) % UNITS, i if v > 0 else i - 1, 0 if first and v == 0 else pair)
                        if behind and g == 0:
                            elu.act_outer_norm(act, t, k)
                        if behind and g == 2:
                            elu.act_own_norm(act, t, k)
                        if behind and g == 3:
                            elu.act_exp(act, t, k)
                        if g == 3 and fin and pair == 1 and hh == 0 and not first:
                            fin.finish(act, (i - BODY) * 2 + k - 2, k)
            both_pairs(act, body, LEAD)
            take_acc(ALL - 1, 1)
            normalise(ALL - 1, UNITS - 1, 2 * BODY - 1, 1)
            if fin:
                for k in range(2):
                    fin.finish(act, T - 2 + k, k)
            else:
                for t in range(T, T + elu.LAG):
                    elu.act_outer_norm(act, t, t % 2)
                    elu.act_own_norm(act, t, t % 2)
                    elu.act_exp(act, t, t % 2)

        @block.tensor
        def _(pe):
            def transposes(u, slot, g):
                n = u * GROUPS + g
                if g == 0:
                    pe.wait_ge(s["e_ready"], u + 1)
                wait(pe, s["pt_ready"], n - 1)
                for q in range(GT):
                    j = g * GT + q
                    mm = nc.tensor.transpose(b.tp[g % 2][:, q * P:(q + 1) * P], b.E[:, slot, j * P:(j + 1) * P],
                                             b.ident[:])
                mm.then_inc(s["t_done"], 1)

            def values(u, v, g, pair):
                pe.wait_ge(s["pt_ready"], u * GROUPS + g + 1)
                if g == 0:
                    wait(pe, s["oT_ready"], u - 1)
                h = 2 * pair + v % 2
                for q in range(GT):
                    j = g * GT + q
                    half = j % 2
                    mm = nc.tensor.matmul(b.bank[4 + v % 2][half * F:(half + 1) * F, 0:P],
                                          b.V[:, j, h * F:(h + 1) * F], b.PT[:, g, q * P:(q + 1) * P],
                                          start=j < 2, stop=j >= T - 2)
                mm.then_inc(s["pv_done"], 1)

            def combine(u, slot):
                pe.wait_ge(s["oT_ready"], u + 1)
                wait(pe, s["out_ready"], u - 1)
                nc.tensor.matmul(b.bank[6 + slot][:, 0:F], b.oT[:, slot, :], b.halves[:], start=True,
                                 stop=True).then_inc(s["o_done"], 1)

            def body(i, pair, first, last):
                for v in range(UNITS):
                    u = i * UNITS + v
                    transposes(u, v % 2, 0)
                    transposes(u, v % 2, 1)
                    if not (first and pair == 0 and v == 0):
                        combine(u - 1, (v - 1) % 2)
                    transposes(u, v % 2, 2)
                    transposes(u, v % 2, 3)
                    for g in range(GROUPS):
                        values(u, v, g, pair)
            both_pairs(pe, body, LEAD)
            combine(ALL - 1, 1)


def row_attention(nc, b, sem, name, layer, x_in, x_out):
    qk = layer == 3
    s = Semaphores(sem, name)
    fin = Finish(nc, b, s, x_in, x_out, half=False)
    pen_t = b.pen_dram.rearrange("(t p) j -> t p j", p=P)
    SPG = GW // SCH
    EXPS = 1 if qk else 2
    X = b.Y if qk else b.E

    with nc.Block() as block:
        @block.sync
        def _(sp):
            def body(i, first, last):
                for k in range(2):
                    tile = i * 2 + k
                    t = sp.snap(tile) if not isinstance(i, int) else tile
                    wait(sp, s["y_ready"], tile - 1)
                    sp.dma_start(b.pen[:, k, :], pen_t[t, :, :]).then_inc(s[f"pen_in{k}"], 16)
                    if qk:
                        ii = sp.snap(i) if not isinstance(i, int) else i
                        wait(sp, s["s_done"], (tile - 1) * GROUPS * SPG)
                        sp.dma_start(b.qT2[:, k, :, :, :].bitcast(F32), b.q_dram[ii, :, :, :, k * P:(k + 1) * P]).then_inc(s[f"q_in{k}"], 16)
            peeled(sp, BODY, body)

        @block.gpsimd
        def _(pool):
            for k in range(2):
                fin.load(pool, k, k)

            def body(i, first, last):
                for k in range(2):
                    u = i * 2 + k
                    if not qk:
                        pool.wait_ge(s["e_ready"], 2 * (u + 1))
                        wait(pool, s["recip"], u - 1)
                        nc.gpsimd.tensor_tensor(b.sums[:, k:k + 1], b.den[:, 2 * k:2 * k + 1],
                                                b.den[:, 2 * k + 1:2 * k + 2], ALU.add).then_inc(s["sums"], 1)
                    if not first:
                        fin.keep(pool, u - 2, k)
                    if not (first and k == 0):
                        fin.add_x(pool, 1 - k, i if k == 1 else i - 1, s["half_out"], u)
                        if not (last and k == 1):
                            pool.wait_ge(s["with_x"], u)
                            fin.load(pool, u + 1, 1 - k)
                        fin.scale_shift(pool, u - 1, 1 - k)
            peeled(pool, BODY, body)
            fin.keep(pool, T - 2, 0)
            fin.add_x(pool, 1, BODY - 1, s["half_out"], T)
            fin.scale_shift(pool, T - 1, 1)
            fin.keep(pool, T - 1, 1)
            for k in range(2):
                pool.wait_ge(s[f"out_kept{k}"], 16 * BODY)

        @block.vector
        def _(dve):
            def scores(i, k, g):
                u = i * 2 + k
                if g == 0:
                    wait(dve, s["e_ready"], EXPS * (u - 1))
                cols = slice(g * GW, (g + 1) * GW)
                nc.vector.scalar_tensor_tensor(b.Y[:, k, cols], b.brow[:, 0, cols], column(b, u, 0),
                                               b.brow[:, 1, cols], ALU.add, ALU.min).then_inc(s["y_raw"], 1)

            def penalised(i, k, g):
                u = i * 2 + k
                if g == 0:
                    if qk:
                        wait(dve, s["t_done"], GROUPS * (u - 1))
                    dve.wait_ge(s[f"pen_in{k}"], 16 * (i + 1))
                    if qk:
                        dg = b.pen[:, k, u * P:(u + 1) * P] if isinstance(u, int) else b.pen[:, k, bass.ds(u * P, P)]
                        nc.vector.tensor_tensor(dg, dg, b.diag_big[:], ALU.subtract).then_inc(s["diag"], 1)
                        dve.wait_ge(s["diag"], u + 1)
                parts = SPG if qk else 1
                for c in range(parts):
                    n = parts * g + c
                    w = GW // parts
                    cols = slice(n * w, (n + 1) * w)
                    if qk:
                        dve.wait_ge(s["s_done"], u * GROUPS * SPG + n + 1)
                    else:
                        dve.wait_ge(s["y_raw"], u * GROUPS + g + 1)
                    dve.sem_inc(b.passed_dve, 1)
                    nc.vector.tensor_tensor_reduce(b.Y[:, k, cols], b.bank[6 + n % 2][:, :] if qk else b.Y[:, k, cols],
                                                   b.pen[:, k, cols], 1.0, 3e38, ALU.add, ALU.min,
                                                   b.ymin8[:, k, n:n + 1]).then_inc(s["part"], 1)
                if g == GROUPS - 1:
                    dve.wait_ge(s["part"], (u + 1) * GROUPS * parts)
                    nc.vector.tensor_reduce(b.ymin[:, k:k + 1], b.ymin8[:, k, 0:GROUPS * parts], AX_X,
                                            ALU.min).then_inc(s["y_ready"], 1)

            def low(u, g):
                n = u * GROUPS + g
                dve.wait_ge(s["h_ready"], n + 1)
                wait(dve, s["pv_done"], n - 1)
                nc.vector.tensor_tensor(b.PL[:, g % 2, :], b.tp[g % 2][:, :], b.PH[:, g % 2, :].bitcast(F32),
                                        ALU.subtract).then_inc(s["l_ready"], 1)

            def recip(u, k):
                if qk:
                    dve.wait_ge(s["e_ready"], u + 1)
                else:
                    dve.wait_ge(s["sums"], u + 1)
                sums = b.den if qk else b.sums
                nc.vector.reciprocal(b.rden[:, k:k + 1], sums[:, k:k + 1]).then_inc(s["recip"], 1)

            def add_low(u, k):
                dve.wait_ge(s["with_x"], u + 1)
                nc.vector.scalar_tensor_tensor(b.out[:, k, :], b.bank[4 + k][:, D:2 * D], b.rden[:, k:k + 1],
                                               b.out[:, k, :], ALU.mult, ALU.add).then_inc(s["out_ready"], 1)

            for k in range(1 if qk else 2):
                for g in range(GROUPS):
                    if not qk:
                        scores(0, k, g)
                    penalised(0, k, g)

            def body(i, first, last):
                for k in range(2):
                    u = i * 2 + k
                    for g in range(GROUPS):
                        if qk and not (last and k == 1):
                            penalised(i + k, 1 - k, g)
                        if not qk and not last:
                            scores(i + 1, k, g)
                        low(u, g)
                        if not qk and not last:
                            penalised(i + 1, k, g)
                        if g == 1:
                            recip(u, k)
                        if not (first and k == 0):
                            if g == 2:
                                add_low(u - 1, 1 - k)
                            if g == 3:
                                fin.moments(dve, u - 1, 1 - k, s["out_ready"], u)
            peeled(dve, BODY, body)
            add_low(T - 1, 1)
            fin.moments(dve, T - 1, 1, s["out_ready"], T)

        @block.scalar
        def _(act):
            def exp(u, k, part=0):
                act.wait_ge(s["y_ready"], u + 1)
                wait(act, s["t_done"], GROUPS * (u - 1))
                wait(act, s["recip"], u - 1)
                cols = slice(part * N // EXPS, (part + 1) * N // EXPS)
                c = EXPS * k + part
                nc.scalar.activation(X[:, k, cols], b.Y[:, k, cols], ACT.Exp, bias=b.ymin[:, k:k + 1], scale=-1.0,
                                     accum_out=b.den[:, c:c + 1]).then_inc(s["e_ready"], 1)

            def normalise(u, k, i):
                act.wait_ge(s["pv_done"], GROUPS * (u + 1))
                act.wait_ge(s["recip"], u + 1)
                wait(act, s[f"out_kept{k}"], 16 * i)
                nc.scalar.activation(b.out[:, k, :], b.bank[4 + k][:, 0:D], ACT.Copy,
                                     scale=b.rden[:, k:k + 1]).then_inc(s["half_out"], 1)

            for part in range(EXPS):
                exp(0, 0, part)

            def body(i, first, last):
                for k in range(2):
                    u = i * 2 + k
                    for g in range(GROUPS):
                        n = u * GROUPS + g
                        act.wait_ge(s["t_done"], n + 1)
                        wait(act, s["pv_done"], n - 1)
                        nc.scalar.activation(b.PH[:, g % 2, :], b.tp[g % 2][:, :], ACT.Copy).then_inc(s["h_ready"], 1)
                        if g == 1 and not first:
                            fin.finish(act, u - 2, k)
                        if g == 1 and not (first and k == 0):
                            normalise(u - 1, 1 - k, i if k == 1 else i - 1)
                        if not qk and g in (1, 2) and not (last and k == 1):
                            exp(u + 1, 1 - k, g - 1)
                    if qk and not (last and k == 1):
                        exp(u + 1, 1 - k)
            peeled(act, BODY, body)
            fin.finish(act, T - 2, 0)
            normalise(T - 1, 1, BODY - 1)
            fin.finish(act, T - 1, 1)

        @block.tensor
        def _(pe):
            def transposes(u, k, g):
                n = u * GROUPS + g
                if g % (GROUPS // EXPS) == 0:
                    pe.wait_ge(s["e_ready"], EXPS * u + g * EXPS // GROUPS + 1)
                wait(pe, s["l_ready"], n - 1)
                for q in range(GT):
                    j = g * GT + q
                    mm = nc.tensor.transpose(b.tp[g % 2][:, q * P:(q + 1) * P], X[:, k, j * P:(j + 1) * P], b.ident[:])
                mm.then_inc(s["t_done"], 1)

            def values(u, k, g):
                pe.wait_ge(s["l_ready"], u * GROUPS + g + 1)
                if g == 0:
                    wait(pe, s["out_ready"], u - 1)
                for q in range(GT):
                    j = g * GT + q
                    cols = slice(q * P, (q + 1) * P)

                    def high_part():
                        return nc.tensor.matmul(b.bank[4 + k][:, 0:2 * D], b.PH[:, g % 2, cols],
                                                b.V2[:, j, :, :].rearrange("p a n -> p (a n)"), start=j == 0, stop=j == T - 1)

                    def low_part():
                        return nc.tensor.matmul(b.bank[4 + k][:, 0:D], b.PL[:, g % 2, cols], b.V2[:, j, 0, :],
                                                start=False, stop=False)
                    if j < T - 1:
                        high_part()
                        mm = low_part()
                    else:
                        low_part()
                        mm = high_part()
                mm.then_inc(s["pv_done"], 1)

            def scores(i, k, c):
                u = i * 2 + k
                if c == 0:
                    pe.wait_ge(s[f"q_in{k}"], 16 * (i + 1))
                wait(pe, s["part"], u * GROUPS * SPG + c - 1)
                cols = slice(c * SCH, (c + 1) * SCH)
                for n, (qp, kp) in enumerate(((0, 0), (0, 1), (1, 0))):
                    for d in range(DC):
                        mm = nc.tensor.matmul(b.bank[6 + c % 2][:, :], b.qT2[:, k, qp, d, :], b.KT2[:, kp, d, cols],
                                              start=n == 0 and d == 0, stop=n == 2 and d == DC - 1)
                mm.then_inc(s["s_done"], 1)

            if qk:
                for c in range(GROUPS * SPG):
                    scores(0, 0, c)
            else:
                for g in range(2):
                    transposes(0, 0, g)

            def body(i, first, last):
                for k in range(2):
                    u = i * 2 + k

                    def next_scores(g):
                        if qk and not (last and k == 1):
                            for c in range(SPG * g, SPG * (g + 1)):
                                scores(i + k, 1 - k, c)
                    if not qk:
                        for g in range(GROUPS):
                            if g < 2:
                                transposes(u, k, g + 2)
                            elif not (last and k == 1):
                                transposes(u + 1, 1 - k, g - 2)
                            values(u, k, g)
                        continue
                    transposes(u, k, 0)
                    next_scores(0)
                    transposes(u, k, 1)
                    next_scores(1)
                    values(u, k, 0)
                    transposes(u, k, 2)
                    next_scores(2)
                    values(u, k, 1)
                    transposes(u, k, 3)
                    next_scores(3)
                    values(u, k, 2)
                    values(u, k, 3)
            peeled(pe, BODY, body)


def graph_layers(nc, x, adj, W0, a1, a2, Wr, br, gamma, beta, W1, a, a_row, Wq, Wk, Wv, out):
    with ExitStack() as ctx:
        def dram(name, shape, dt=F32):
            return nc.dram_tensor(name, shape, dt, kind="Internal").ap()

        def sb(scope, name, shape, dt=F32):
            return scope.enter_context(nc.sbuf_tensor(name, shape, dt))

        b = Buffers()
        b.passed_dve = ctx.enter_context(nc.semaphore("passed_dve"))
        b.passed_pool = ctx.enter_context(nc.semaphore("passed_pool"))
        b.adj = adj
        b.pen_dram = dram("pen_dram", (N, N), BF16)
        b.o_dram = dram("o_dram", (N, D))
        b.res_dram = dram("res_dram", (N, D))
        b.rows_dram = dram("rows_dram", (2 * HEADS, N))
        b.q_dram = dram("q_dram", (BODY, P, 2, DC, 2 * P), F32)
        x1, x2, x3 = (dram(f"x{n}_dram", (N, D)) for n in (1, 2, 3))

        psum = ctx.enter_context(nc.psum_tensor("psum", [P, 8, 512], F32))
        b.bank = [psum[:, k, :] for k in range(8)]
        b.tp = [psum[:, 2 * k:2 * k + 2, :].rearrange("p a n -> p (a n)") for k in range(2)]

        b.ident = sb(ctx, "ident", [P, P])
        b.halves = sb(ctx, "halves", [P, F])
        b.diag_big = sb(ctx, "diag_big", [P, P], BF16)
        b.big_col = sb(ctx, "big_col", [P, 1])
        b.minus_half = sb(ctx, "minus_half", [P, 1])
        b.col = sb(ctx, "col", [P, T, HEADS])
        b.Y = sb(ctx, "Y", [P, 2, N])
        b.pen = sb(ctx, "pen", [P, 2, N], BF16)
        b.out = sb(ctx, "out_tile", [P, 2, D])
        b.ymin = sb(ctx, "ymin", [P, 4])
        b.moments = sb(ctx, "moments", [P, 2, 6])
        b.row_stats = sb(ctx, "row_stats", [P, 2, 6])
        b.ymin8 = sb(ctx, "ymin8", [P, 2, N // SCH])
        b.den, b.rden, b.lone, b.sums = (sb(ctx, n, [P, 4]) for n in ("den", "rden", "lone", "sums"))

        def parts(buffer, *shapes):
            whole = buffer[:].rearrange("p a n -> p (a n)")
            at, cut = 0, []
            for shape in shapes:
                size = 1
                for n in shape:
                    size *= n
                ap = whole[:, at:at + size]
                at += size
                if len(shape) > 1:
                    letters = "abcd"[:len(shape)]
                    ap = ap.rearrange(f"p ({' '.join(letters)}) -> p {' '.join(letters)}", **dict(zip(letters, shape)))
                cut.append(ap)
            return cut

        (b.xs, b.xT, b.row_tile, b.wx, b.wrow, b.wsum, b.wq, b.wk) = parts(
            b.Y, (2, 2, D), (2, DC, 2 * P), (2, 2 * P), (DC, D + HEADS),
            (DC, 2 * HEADS), (DC, 2, HEADS), (DC, D), (DC, D))
        taken = []

        def sem(name):
            taken.append(nc.alloc_semaphore(name=name))
            return taken[-1]

        def stage(make, *args):
            make(nc, b, sem, *args)
            nc.clear_and_free_semaphores(taken)
            nc.all_engine_barrier()
            taken.clear()

        stage(constants)
        with ExitStack() as gat:
            b.brow = sb(gat, "brow", [P, 4, N])
            b.V = sb(gat, "V", [P, T, D])
            b.E = sb(gat, "E", [P, 2, N])
            b.PT = sb(gat, "PT", [P, GROUPS, GW])
            b.oT = sb(gat, "oT", [P, 2, P])
            b.res_tile, b.wres, b.br, b.avec, b.wprod = parts(b.E, (2, 2, D), (DC, D), (D,), (2, D), (D,))
            stage(gat_weights, "g0", W0, a2, a1)
            stage(dense_weights, "d0", [(b.wres, Wr), (b.br, br)])
            stage(tiles_of_rows, "r0", x, "gat", True)
            with nc.sbuf_tensor("adj_chunk", [P, 2, GW], I32) as b.adj_chunk:
                b.gamma, b.beta, b.x_one, b.res, b.elu, b.sum, b.o_half = parts(
                    b.adj_chunk.bitcast(F32), (D,), (D,), (D,), (D,), (D,), (2, D), (D // 2,))
                stage(gat_attention, "a0", 0, x, x1, gamma, beta)
            stage(gat_weights, "g1", W1, a[:, 0:F], a[:, F:2 * F])
            stage(tiles_of_rows, "r1", x1, "gat")
            with nc.sbuf_tensor("x_tile1", [P, 2, D], F32) as b.x_tile, \
                    nc.sbuf_tensor("o_half1", [P, 2, D // 2], F32) as b.o_half:
                stage(gat_attention, "a1", 1, x1, x2)
        with ExitStack() as row:
            b.brow = sb(row, "brow2", [P, 2, N])
            b.V2 = sb(row, "V2", [P, T, 2, D], F32R)
            b.E = sb(row, "E2", [P, 2, N])
            b.PH, b.PL = (sb(row, n, [P, 2, GW], F32R) for n in ("PH2", "PL2"))
            stage(row_weights, "g2", a_row)
            b.x_tile = sb(row, "x_tile2", [P, 2, D])
            stage(tiles_of_rows, "r2", x2, "row")
            stage(row_attention, "a2", 2, x2, x3)
        with ExitStack() as qkv:
            b.KT2 = sb(qkv, "KT3", [P, 2, DC, N], F32R)
            b.V2 = sb(qkv, "V3", [P, T, 2, D], F32R)
            b.PH, b.PL = (sb(qkv, n, [P, 2, GW], F32R) for n in ("PH3", "PL3"))
            b.qT2 = sb(qkv, "qT3", [P, 2, 2, DC, P], F32R)
            b.q_stage = b.PH[:].rearrange("p a (h c n) -> p a h c n", h=2, c=DC)
            stage(dense_weights, "g3", [(b.wx[:, :, 0:D], Wv), (b.wq, Wq), (b.wk, Wk)])
            b.x_tile = sb(qkv, "x_tile3", [P, 2, D])
            stage(tiles_of_rows, "r3", x3, "qkv")
            stage(row_attention, "a3", 3, x3, out)


_INS = ["x", "adj", "L0_gnn_W", "L0_gnn_a1", "L0_gnn_a2", "L0_gnn_Wr", "L0_gnn_br", "L0_gnn_gamma", "L0_gnn_beta",
        "L1_gnn_W", "L1_gnn_a", "L2_gnn_a", "L3_gnn_Wq", "L3_gnn_Wk", "L3_gnn_Wv"]
_OUTS = [((N, D), "float32")]


def kernel(**inputs):
    import numpy as _np
    import concourse.bacc as _bacc
    from concourse import mybir as _mybir
    from concourse.bass_utils import run_bass_kernel_spmd as _run

    nc = _bacc.Bacc("TRN2", target_bir_lowering=False, num_devices=1)
    arrays, args = {}, []
    for name in _INS:
        v = _np.ascontiguousarray(inputs[name])
        arrays[f"in_{name}_dram"] = v
        args.append(nc.dram_tensor(f"in_{name}_dram", v.shape, _mybir.dt.from_np(v.dtype), kind="ExternalInput").ap())
    for i, (shape, dtype) in enumerate(_OUTS):
        dt = _mybir.dt.from_np(_np.dtype(dtype))
        args.append(nc.dram_tensor(f"out_{i}_dram", shape, dt, kind="ExternalOutput").ap())
    graph_layers(nc, *args)
    r = _run(nc, [arrays], core_ids=[0])
    return r.results[0]["out_0_dram"]
```
